# Optimizing a Trainium2 kernel written in Bass

```python
import numpy as np
import jax
import jax.numpy as jnp

def _softmax(x, axis=-1):
    return jax.nn.softmax(x, axis=axis)

def _gelu(x):
    return jax.nn.gelu(x, approximate=True)

def _silu(x):
    return jax.nn.silu(x)

def _sigmoid(x):
    return jax.nn.sigmoid(x)

def _layernorm(x, axis=-1, eps=1e-05):
    m = jnp.mean(x, axis=axis, keepdims=True)
    v = jnp.var(x, axis=axis, keepdims=True)
    return (x - m) / jnp.sqrt(v + eps)

def _scatter_add(tgt, idx, src, axis=0):
    return tgt.at[idx].add(src)

def _segment_sum(src, seg, n):
    return jax.ops.segment_sum(src, seg, n)
kernel_name = 'mk_macaron_d1_jaxref_r8_1c9702'

def setup_inputs(seed: int=0):
    np.random.seed(seed)
    _w = jnp.asarray

    def _L0_attn_setup():
        import jax, jax.numpy as jnp
        import numpy as np
        DIM_Q = 128
        DIM_K = 128
        DIM_V = 128
        OUT_DIM = 128
        B, N = (4, 256)

        def _layer_norm(h, gamma, beta, eps=1e-05):
            mu = jnp.mean(h, axis=-1, keepdims=True)
            var = jnp.mean(jnp.square(h - mu), axis=-1, keepdims=True)
            return (h - mu) * jax.lax.rsqrt(var + eps) * gamma + beta
        key = jax.random.key(seed)
        ks = jax.random.split(key, 8)
        s_in = 1.0 / np.sqrt(DIM_Q)
        s_v = 1.0 / np.sqrt(DIM_V)
        return {'x': jax.random.normal(ks[0], (B, N, DIM_Q), dtype=jnp.float32), 'Wq': jax.random.normal(ks[1], (DIM_Q, DIM_K), dtype=jnp.float32) * s_in, 'Wk': jax.random.normal(ks[2], (DIM_Q, DIM_K), dtype=jnp.float32) * s_in, 'Wv': jax.random.normal(ks[3], (DIM_Q, DIM_V), dtype=jnp.float32) * s_in, 'Wfc': jax.random.normal(ks[4], (DIM_V, OUT_DIM), dtype=jnp.float32) * s_v, 'bfc': jax.random.normal(ks[5], (OUT_DIM,), dtype=jnp.float32) * 0.02, 'gamma': jnp.ones((DIM_V,), dtype=jnp.float32), 'beta': jnp.zeros((DIM_V,), dtype=jnp.float32)}
    _L0_attn_in = _L0_attn_setup()

    def _L0_ffn_setup():
        import jax, jax.numpy as jnp
        import numpy as np
        TOP_K = 2
        EPS = 1e-09
        key = jax.random.key(seed)
        ks = jax.random.split(key, 6)
        B, T, D, H, E = (4, 256, 128, 256, 8)
        x = jax.random.normal(ks[0], (B, T, D), dtype=jnp.float32)
        Wg = jax.random.normal(ks[1], (E, D), dtype=jnp.float32) * 0.02
        W1 = jax.random.normal(ks[2], (E, 2 * H, D), dtype=jnp.float32) * 0.02
        b1 = jax.random.normal(ks[3], (E, 2 * H), dtype=jnp.float32) * 0.02
        Wo = jax.random.normal(ks[4], (D, H), dtype=jnp.float32) * 0.02
        bo = jax.random.normal(ks[5], (D,), dtype=jnp.float32) * 0.02
        return {'x': x, 'Wg': Wg, 'W1': W1, 'b1': b1, 'Wo': Wo, 'bo': bo}
    _L0_ffn_in = _L0_ffn_setup()
    _d = {'L0_attn_x': _L0_attn_in['x'], 'L0_attn_Wq': _L0_attn_in['Wq'], 'L0_attn_Wk': _L0_attn_in['Wk'], 'L0_attn_Wv': _L0_attn_in['Wv'], 'L0_attn_Wfc': _L0_attn_in['Wfc'], 'L0_attn_bfc': _L0_attn_in['bfc'], 'L0_attn_gamma': _L0_attn_in['gamma'], 'L0_attn_beta': _L0_attn_in['beta'], 'L0_ffn_Wg': _L0_ffn_in['Wg'], 'L0_ffn_W1': _L0_ffn_in['W1'], 'L0_ffn_b1': _L0_ffn_in['b1'], 'L0_ffn_Wo': _L0_ffn_in['Wo'], 'L0_ffn_bo': _L0_ffn_in['bo']}
    _x0 = _d['L0_attn_x']
    _d['L0_attn_x'] = jax.random.normal(jax.random.fold_in(jax.random.key(seed), 1), (4, 1024, 128), dtype=_x0.dtype)
    del _x0
    return _d

def reference(L0_attn_x, L0_attn_Wq, L0_attn_Wk, L0_attn_Wv, L0_attn_Wfc, L0_attn_bfc, L0_attn_gamma, L0_attn_beta, L0_ffn_Wg, L0_ffn_W1, L0_ffn_b1, L0_ffn_Wo, L0_ffn_bo):

    def _L0_attn_ref(x, Wq, Wk, Wv, Wfc, bfc, gamma, beta):
        import jax, jax.numpy as jnp
        import numpy as np
        DIM_Q = 128
        DIM_K = 128
        DIM_V = 128
        OUT_DIM = 128
        B, N = (4, 256)

        def _layer_norm(h, gamma, beta, eps=1e-05):
            mu = jnp.mean(h, axis=-1, keepdims=True)
            var = jnp.mean(jnp.square(h - mu), axis=-1, keepdims=True)
            return (h - mu) * jax.lax.rsqrt(var + eps) * gamma + beta
        q = jnp.einsum('bnd,dk->bnk', x, Wq)
        k = jnp.einsum('bnd,dk->bnk', x, Wk)
        v = jnp.einsum('bnd,dv->bnv', x, Wv)
        scale = 1.0 / np.sqrt(DIM_K)
        scores = jnp.einsum('bnk,bmk->bnm', q, k) * scale
        n = x.shape[1]
        causal = jnp.tril(jnp.ones((n, n), dtype=bool))
        scores = jnp.where(causal, scores, -jnp.inf)
        att = jax.nn.softmax(scores, axis=-1)
        out = jnp.einsum('bnm,bmv->bnv', att, v)
        out = _layer_norm(out + v, gamma, beta)
        return jnp.einsum('bnv,vo->bno', out, Wfc) + bfc

    def _L0_ffn_ref(x, Wg, W1, b1, Wo, bo):
        import jax, jax.numpy as jnp
        import numpy as np
        TOP_K = 2
        EPS = 1e-09
        E = Wg.shape[0]
        gate_logits = jnp.einsum('btd,ed->bte', x, Wg)
        gate_scores = jax.nn.softmax(gate_logits, axis=-1)
        topk_val, topk_idx = jax.lax.top_k(gate_scores, TOP_K)
        topk_val = topk_val / (topk_val.sum(axis=-1, keepdims=True) + EPS)
        comb = (jax.nn.one_hot(topk_idx, E, dtype=x.dtype) * topk_val[..., None]).sum(axis=-2)
        out = jnp.zeros_like(x)
        for e in range(E):
            h = jnp.einsum('btd,hd->bth', x, W1[e]) + b1[e]
            a, b = jnp.split(h, 2, axis=-1)
            g = a * jax.nn.sigmoid(b)
            eo = jnp.einsum('bth,dh->btd', g, Wo) + bo
            out = out + eo * comb[..., e:e + 1]
        return out
    x = L0_attn_x
    x = x + 0.5 * _L0_ffn_ref(_layernorm(x, axis=-1), L0_ffn_Wg, L0_ffn_W1, L0_ffn_b1, L0_ffn_Wo, L0_ffn_bo)
    x = x + _L0_attn_ref(_layernorm(x, axis=-1), L0_attn_Wq, L0_attn_Wk, L0_attn_Wv, L0_attn_Wfc, L0_attn_bfc, L0_attn_gamma, L0_attn_beta)
    x = x + 0.5 * _L0_ffn_ref(_layernorm(x, axis=-1), L0_ffn_Wg, L0_ffn_W1, L0_ffn_b1, L0_ffn_Wo, L0_ffn_bo)
    return x

_drawn_inputs = setup_inputs


def setup_inputs(seed=0):
    import zlib

    import numpy as np

    out = dict(_drawn_inputs(seed))
    spreads = {'L0_attn_gamma': (1.0, 0.2), 'L0_attn_beta': (0.0, 0.1)}
    factors = {'L0_attn_bfc': 3.532,
     'L0_ffn_Wg': 3.706,
     'L0_ffn_W1': 3.194,
     'L0_ffn_b1': 8.0,
     'L0_ffn_Wo': 3.161}
    for name, (base, spread) in spreads.items():
        noise = np.random.default_rng([zlib.crc32(name.encode()), seed]).standard_normal(out[name].shape)
        drawn = base * np.exp(spread * noise) if base else spread * noise
        out[name] = jnp.asarray(drawn.astype(out[name].dtype))
    for name, factor in factors.items():
        out[name] = (out[name] * factor).astype(out[name].dtype)
    return out
```

```python
from contextlib import ExitStack

import concourse.bass as bass
from concourse import mybir

F32 = mybir.dt.float32
F32R = mybir.dt.float32r
U32 = mybir.dt.uint32
ALU = mybir.AluOpType
ACT = mybir.ActivationFunctionType
AX = mybir.AxisListType

P = 128
LN_EPS = 1e-05
TOPK_EPS = 1e-09
MASKED = -1e30
CREDIT = 1


class Chain:

    def __init__(self, eng, sem):
        self.eng, self.sem, self.base, self.n = eng, sem, 0, 0

    def step(self, ins):
        ins.then_inc(self.sem, 1)
        self.n += 1

    def wait(self):
        self.eng.wait_ge(self.sem, self.base + self.n)


def wait_for(eng, sem, count):
    if not (isinstance(count, int) and count <= 0):
        eng.wait_ge(sem, count)


def pT_count(n):
    return sum(t // 4 + 1 for t in range(max(n, 0)))


def pv_before(g):
    n = 0
    while pT_count(n + 1) <= g:
        n += 1
    return n + 1


def macaron_kernel(nc, x_in, wq, wk, wv, wfc, bfc, gamma, beta, wg, w1, b1, wo, bo, out):
    B, N, D = x_in.shape
    E, H2, _ = w1.shape
    H = H2 // 2
    HC = H // P
    TILES = B * N // P
    MT = 4
    MACROS = TILES // MT
    BT = N // P
    SCALE = 1.0 / float(D) ** 0.5
    assert D == P and H2 == 512 and E == 8 and BT == 2 * MT

    x_tiles = x_in.rearrange("b (t p) d -> p (b t) d", p=P)
    out_tiles = out.rearrange("b (t p) d -> p (b t) d", p=P)

    with ExitStack() as ctx:
        def sb(name, shape, dt=F32):
            return ctx.enter_context(nc.sbuf_tensor(name, shape, dt))

        def ps(name, shape):
            return ctx.enter_context(nc.psum_tensor(name, shape, F32))

        def sem(name):
            return ctx.enter_context(nc.semaphore(name))

        x = sb("x", [P, TILES, D])
        ident = sb("ident", [P, P])
        ident_r = sb("ident_r", [P, P], F32R)
        causal_f = sb("causal_f", [P, P])
        causal_r = sb("causal_r", [P, P], F32R)
        expert_no = sb("expert_no", [P, MT, E])
        minus_half = sb("minus_half", [P, MT])
        ln_eps = sb("ln_eps", [P, MT])
        bo_rows = sb("bo_rows", [P, D])
        bfc_rows = sb("bfc_rows", [P, D])
        gamma_col = sb("gamma_col", [P, 1])
        beta_col = sb("beta_col", [P, 1])
        w1_rows = sb("w1_rows", [P, E * MT, D])
        b1_rows = sb("b1_rows", [E * MT, P])
        wg_rows = sb("wg_rows", [E, D])
        wo_rows = sb("wo_rows", [D, H])
        sq_raw = sb("sq_raw", [P, 4, D])
        w1_h = sb("w1_h", [P, E, H2], F32R)
        w1_l = sb("w1_l", [P, E, H2], F32R)
        wg_h = sb("wg_h", [P, E], F32R)
        wg_l = sb("wg_l", [P, E], F32R)
        wo_h = sb("wo_h", [P, HC, D], F32R)
        wo_l = sb("wo_l", [P, HC, D], F32R)
        sq_h = sb("sq_h", [P, 4, D], F32R)
        sq_l = sb("sq_l", [P, 4, D], F32R)
        stats = sb("stats", [P, MT, 6])
        wait_carrier = sb("wait_carrier", [P, 1])
        mean_var = sb("mean_var", [P, MT, 2])
        var_eps = sb("var_eps", [P, MT])
        rstd = sb("rstd", [P, MT])
        xn = sb("xn", [P, MT, D])
        xn_full = sb("xn_full", [P, MT, D])
        xT_h = sb("xT_h", [P, 2, MT * P], F32R)
        xT_l = sb("xT_l", [P, 2, MT * P], F32R)
        logits = sb("logits", [P, MT, E])
        top8 = sb("top8", [P, MT, 8])
        top_at = sb("top_at", [P, MT, 8], U32)
        below_max = sb("below_max", [P, MT, E])
        sig_pos = sb("sig_pos", [P, MT, E])
        sig_neg = sb("sig_neg", [P, MT, E])
        expo = sb("expo", [P, MT, E])
        is_first = sb("is_first", [P, MT, E])
        is_second = sb("is_second", [P, MT, E])
        z_all = sb("z_all", [P, MT])
        z_top = sb("z_top", [P, MT])
        z_den = sb("z_den", [P, MT])
        comb = sb("comb", [P, 2, MT, E])
        comb_sum = sb("comb_sum", [P, 2, MT])
        gate = sb("gate", [P, 2, 2, H])
        gated = sb("gated", [P, 2, E // 2, 2 * H])
        g_sum = sb("g_sum", [P, 2, H])
        gT_h = sb("gT_h", [P, HC * P], F32R)
        gT_l = sb("gT_l", [P, HC * P], F32R)
        resid = sb("resid", [P, 2, D])
        q_h = sb("q_h", [P, N], F32R)
        q_l = sb("q_l", [P, N], F32R)
        k_h = sb("k_h", [P, N], F32R)
        k_l = sb("k_l", [P, N], F32R)
        v_h = sb("v_h", [P, BT, D], F32R)
        v_l = sb("v_l", [P, BT, D], F32R)
        v_f = sb("v_f", [P, BT, D])
        row_max = sb("row_max", [P, BT])
        neg_max = sb("neg_max", [P, BT])
        row_sum = sb("row_sum", [P, BT])
        row_inv = sb("row_inv", [P, BT])
        probs = sb("probs", [P, 2, N])
        pT_h = sb("pT_h", [P, 2, MT * P], F32R)
        pT_l = sb("pT_l", [P, 2, MT * P], F32R)
        y = sb("y", [P, MT, D])
        y_stats = sb("y_stats", [P, MT, 6])
        y_mean_var = sb("y_mean_var", [P, MT, 2])
        y_var_eps = sb("y_var_eps", [P, MT])
        y_rstd = sb("y_rstd", [P, MT])
        yn = sb("yn", [P, MT, D])
        yT = sb("yT", [P, MT * P])
        yT_h = sb("yT_h", [P, MT * P], F32R)
        yT_l = sb("yT_l", [P, MT * P], F32R)
        x_bfc = sb("x_bfc", [P, MT, D])

        ps_h = ps("ps_h", [P, 4, 512])
        ps_t = ps("ps_t", [P, 512])
        ps_lg = ps("ps_lg", [P, 512])
        ps_g = ps("ps_g", [P, 512])
        ps_y = ps("ps_y", [P, 512])
        ps_p = [ps_lg, ps_g]

        names = """x_first x_rest w1_in b1_in small_in sq_in rows_in const_id const_ones iota_done wprep
            w1_sub w_tp w_hi w_lo b1_t b1_put sq_hi sq_lo setup_dve
            stat_done rstd_done xn_done xT_done xh_done xl_done lg_done lgc_done below_done sig_done comb_done
            h_done gate_done gated_done gsum_done gT_done gh_done gl_done y_done x_done
            a_stat a_rstd a_xn a_xT a_xh a_xl pj_done pj_hi pj_lo vf_done sc_done max_done exp_done
            pT_done ph_done pl_done pv_done yrow_done y_stat y_rs yn_done yT_done yt_done yh_done yl_done
            fc_done xb_done xa_done out_done dve_chain pool_chain""".split()
        S = {n: sem(n) for n in names}
        block = ctx.enter_context(nc.Block())

        @block.sync
        def _(sp):
            sp.dma_start(x[:, 0:MT, :], x_tiles[:, 0:MT, :]).then_inc(S["x_first"], 16)
            w1_blocks = w1.rearrange("e (j p) d -> p (e j) d", p=P)
            sp.dma_start(w1_rows[:, 0:E * MT // 2, :], w1_blocks[:, 0:E * MT // 2, :]).then_inc(S["w1_in"], 16)
            sp.dma_start(w1_rows[:, E * MT // 2:, :], w1_blocks[:, E * MT // 2:, :]).then_inc(S["w1_in"], 16)
            sp.dma_start(x[:, MT:TILES, :], x_tiles[:, MT:TILES, :]).then_inc(S["x_rest"], 16)
            for m in range(MACROS):
                sp.wait_ge(S["x_done"], CREDIT + TILES + MT * (m + 1))
                sp.dma_start(out_tiles[:, m * MT:(m + 1) * MT, :], x[:, m * MT:(m + 1) * MT, :])\
                    .then_inc(S["out_done"], 16)
            sp.wait_ge(S["out_done"], 16 * MACROS)

        def pool_rstd(pool, chain, var, eps_out, result, done):
            chain.step(pool.tensor_tensor(eps_out, var, ln_eps[:, :], ALU.add))
            chain.wait()
            pool.tensor_tensor(result, eps_out, minus_half[:, :], ALU.pow).then_inc(done, 1)

        def dve_stats(dve, chain, rows, st, mv, done):
            for t in range(MT):
                chain.step(dve.bn_stats(st[:, t, :], rows(t)))
            chain.wait()
            dve.tensor_copy(wait_carrier[:, :], st[:, 0, 0:1])
            for t in range(MT):
                last = dve.bn_aggr(mv[:, t, :], st[:, t, :])
            last.then_inc(done, 1)

        def ffn_steps(eng, phase, step, chain=None):
            t0 = phase * TILES
            step(0, t0, t0 // MT, None)
            start = chain.n if chain else 0
            with eng.Fori(0, TILES // 8 - 1) as i:
                if chain:
                    per = chain_per_loop[chain.sem.name]
                    chain.base, chain.n = start + i * per, 0
                for k in range(1, 9):
                    m = t0 // MT + i * 2 + k // MT
                    step(k, t0 + i * 8 + k, m, i * 2 + (k // MT + 1) if k < 8 else None)
                if chain:
                    assert chain.n == per, (chain.sem.name, chain.n)
            if chain:
                chain.base, chain.n = 0, start + (TILES // 8 - 1) * per
            for k in range(1, 8):
                m0 = (TILES // 8 - 1) * 2 + k // MT
                step(k, t0 + TILES - 8 + k, t0 // MT + m0, m0 + 1 if k < MT else None)

        chain_per_loop = {"dve_chain": 8 + 2 * 15, "pool_chain": 8 * 3 + 2}

        @block.gpsimd
        def _(pool):
            chain = Chain(pool, S["pool_chain"])
            for name in ("gsum_done", "vf_done"):
                pool.sem_inc(S[name], CREDIT)
            pool.dma_start(b1_rows[:, :], b1.rearrange("e (j p) -> (e j) p", p=P)).then_inc(S["b1_in"], 16)
            pool.memset(ident[:, :], 0.0).then_inc(S["const_id"], 1)
            pool.memset(causal_f[:, :], 0.0).then_inc(S["const_id"], 1)
            pool.wait_ge(S["const_id"], 2)
            pool.affine_select(out=ident[:, :], in_=ident[:, :], compare_op=ALU.not_equal, fill=1.0, base=0,
                               pattern=[[-1, P]], channel_multiplier=1).then_inc(S["const_id"], 1)
            pool.affine_select(out=causal_f[:, :], in_=causal_f[:, :], compare_op=ALU.is_ge, fill=MASKED, base=0,
                               pattern=[[-1, P]], channel_multiplier=1).then_inc(S["const_id"], 1)
            pool.memset(minus_half[:, :], -0.5).then_inc(S["const_ones"], 1)
            pool.memset(ln_eps[:, :], LN_EPS).then_inc(S["const_ones"], 1)
            for e in range(E):
                pool.memset(expert_no[:, :, e:e + 1], float(e)).then_inc(S["iota_done"], 1)
            pool.wait_ge(S["const_ones"], 2)

            def prep(mg):
                pool.wait_ge(S["stat_done"], mg + 1)
                wait_for(pool, S["xn_done"], mg)
                pool_rstd(pool, chain, mean_var[:, :, 1], var_eps[:, :], rstd[:, :], S["rstd_done"])

            prep(0)
            for hf in range(2):
                pool.wait_ge(S["w1_in"], 32)
                lo, hi = hf * E * MT // 2, (hf + 1) * E * MT // 2
                pool.tensor_tensor(w1_rows[:, lo:hi, 0:D - 1], w1_rows[:, lo:hi, 0:D - 1],
                                   w1_rows[:, lo:hi, D - 1:D].to_broadcast([P, hi - lo, D - 1]),
                                   ALU.subtract).then_inc(S["w1_sub"], 1)

            def step(k, tg, mg, nxt):
                if k in (1, 4) and nxt is not None:
                    prep(mg + 1)
                g = gated[:, k % 2]
                pool.wait_ge(S["gated_done"], 4 * tg + 2)
                chain.step(pool.tensor_tensor(g[:, 0, :], g[:, 0, :], g[:, 1, :], ALU.add))
                pool.wait_ge(S["gated_done"], 4 * tg + 4)
                chain.step(pool.tensor_tensor(g[:, 2, :], g[:, 2, :], g[:, 3, :], ALU.add))
                chain.wait()
                chain.step(pool.tensor_tensor(g[:, 0, :], g[:, 0, :], g[:, 2, :], ALU.add))
                chain.wait()
                wait_for(pool, S["gT_done"], CREDIT + tg - 1)
                pool.tensor_tensor(g_sum[:, k % 2, :], g[:, 0, 0:H], g[:, 0, H:2 * H], ALU.add)\
                    .then_inc(S["gsum_done"], 1)

            ffn_steps(pool, 0, step, chain)

            at_start = chain.n
            PER = 4
            pool.wait_ge(S["x_done"], CREDIT + TILES)
            with pool.Fori(0, B) as b:
                chain.base, chain.n = at_start + b * PER, 0
                for j in range(2):
                    pool.wait_ge(S["a_stat"], 2 * b + j + 1)
                    pool.wait_ge(S["a_xn"], CREDIT + 2 * b + j)
                    pool_rstd(pool, chain, mean_var[:, :, 1], var_eps[:, :], rstd[:, :], S["a_rstd"])
                for j in range(2):
                    pool.wait_ge(S["pj_lo"], 6 * b + 3 * j + 3)
                    pool.wait_ge(S["xa_done"], CREDIT + 2 * b)
                    ts = slice(j * MT, (j + 1) * MT)
                    pool.tensor_tensor(v_f[:, ts, :], v_h[:, ts, :].bitcast(F32), v_l[:, ts, :].bitcast(F32), ALU.add)\
                        .then_inc(S["vf_done"], 1)
                for j in range(2):
                    pool.wait_ge(S["xa_done"], CREDIT + 2 * b + j)
                    pool.tensor_tensor(x_bfc[:, :, :], x[:, bass.ds(b * BT + j * MT, MT), :],
                                       bfc_rows[:, None, :].to_broadcast([P, MT, D]), ALU.add)\
                        .then_inc(S["xb_done"], 1)
                    pool.wait_ge(S["y_stat"], 2 * b + j + 1)
                    pool.wait_ge(S["yn_done"], CREDIT + 2 * b + j)
                    pool_rstd(pool, chain, y_mean_var[:, :, 1], y_var_eps[:, :], y_rstd[:, :], S["y_rs"])
                assert chain.n == PER
            chain.base, chain.n = 0, at_start + B * PER

            prep(MACROS)
            ffn_steps(pool, 1, step, chain)

        @block.scalar
        def _(act):
            for name in ("exp_done", "yh_done"):
                act.sem_inc(S[name], CREDIT)
            act.dma_start(wg_rows[:, :], wg).then_inc(S["small_in"], 16)
            act.dma_start(wo_rows[:, :], wo).then_inc(S["small_in"], 16)
            for n, w in enumerate((wq, wk, wv, wfc)):
                act.dma_start(sq_raw[:, n, :], w).then_inc(S["sq_in"], 16)
            act.dma_start(bo_rows[:, :], bo.rearrange("(a d) -> a d", a=1).to_broadcast([P, D]))\
                .then_inc(S["rows_in"], 16)
            act.dma_start(bfc_rows[:, :], bfc.rearrange("(a d) -> a d", a=1).to_broadcast([P, D]))\
                .then_inc(S["rows_in"], 16)
            act.dma_start(gamma_col[:, :], gamma.rearrange("(p a) -> p a", a=1)).then_inc(S["rows_in"], 16)
            act.dma_start(beta_col[:, :], beta.rearrange("(p a) -> p a", a=1)).then_inc(S["rows_in"], 16)

            def xh(mg, parity):
                act.wait_ge(S["xT_done"], mg + 1)
                if not (isinstance(mg, int) and mg < 2):
                    act.wait_ge(S["h_done"], CREDIT + 16 * mg - 16)
                act.activation(xT_h[:, parity, :], ps_t[:, :], ACT.Copy).then_inc(S["xh_done"], 1)

            def sigmoids(mg):
                act.wait_ge(S["below_done"], mg + 1)
                wait_for(act, S["comb_done"], mg)
                act.activation(sig_pos[:, :, :], below_max[:, :, :], ACT.Sigmoid)
                act.activation(sig_neg[:, :, :], below_max[:, :, :], ACT.Sigmoid, scale=-1.0)\
                    .then_inc(S["sig_done"], 1)

            def pair(k, tg, q):
                n = 4 * tg + q
                act.wait_ge(S["h_done"], CREDIT + n + 1)
                wait_for(act, S["gated_done"], n - 1)
                s = 2 * (q % 2)
                act.activation(gate[:, q % 2, :, :], ps_h[:, s:s + 2, H:2 * H], ACT.Sigmoid)\
                    .then_inc(S["gate_done"], 1)

            def gh(tg):
                act.wait_ge(S["gT_done"], CREDIT + tg + 1)
                wait_for(act, S["y_done"], CREDIT + tg)
                act.activation(gT_h[:, :], ps_g[:, 0:HC * P], ACT.Copy).then_inc(S["gh_done"], 1)

            def step(k, tg, mg, nxt):
                for q in range(4):
                    pair(k, tg, q)
                    if q == 2 and k > 0:
                        gh(tg - 1)
                if nxt is not None:
                    if k in (2, 5):
                        xh(mg + 1, (k // MT + 1) % 2)
                    if k in (3, 7):
                        sigmoids(mg + 1)

            xh(0, 0)
            for e in range(E):
                act.wait_ge(S["w_tp"], e + 1)
                act.activation(w1_h[:, e, :], ps_h[:, e % 4, :], ACT.Copy).then_inc(S["w_hi"], 1)
            act.wait_ge(S["w_tp"], E + 1)
            act.activation(wg_h[:, :], ps_lg[:, 0:E], ACT.Copy).then_inc(S["w_hi"], 1)
            act.wait_ge(S["w_tp"], E + 2)
            act.activation(wo_h[:, :, :], ps_y[:, 0:HC * D].rearrange("p (c d) -> p c d", c=HC), ACT.Copy)\
                .then_inc(S["w_hi"], 1)
            act.wait_ge(S["sq_in"], 64)
            act.activation(sq_h[:, :, :], sq_raw[:, :, :], ACT.Copy).then_inc(S["sq_hi"], 1)
            act.wait_ge(S["const_id"], 4)
            act.activation(ident_r[:, :], ident[:, :], ACT.Copy).then_inc(S["sq_hi"], 1)
            act.activation(causal_r[:, :], causal_f[:, :], ACT.Copy).then_inc(S["sq_hi"], 1)
            sigmoids(0)
            ffn_steps(act, 0, step)
            gh(TILES - 1)

            act.wait_ge(S["h_done"], CREDIT + 4 * TILES)
            with act.Fori(0, B) as b:
                for j in range(2):
                    act.wait_ge(S["a_xT"], CREDIT + 2 * b + j + 1)
                    act.wait_ge(S["pj_done"], CREDIT + 6 * b)
                    act.activation(xT_h[:, j, :], ps_t[:, :], ACT.Copy).then_inc(S["a_xh"], 1)
                for j in range(2):
                    for c, dst in enumerate((q_h, k_h, v_h)):
                        u = 3 * j + c
                        act.wait_ge(S["pj_done"], CREDIT + 6 * b + u + 1)
                        act.wait_ge(S["pv_done"], CREDIT + 8 * b)
                        if c == 2:
                            act.wait_ge(S["vf_done"], CREDIT + 2 * b)
                        d = dst[:, j * 512:(j + 1) * 512] if c < 2 else \
                            dst[:, j * MT:(j + 1) * MT, :].rearrange("p t d -> p (t d)")
                        act.activation(d, ps_h[:, u % 4, :], ACT.Copy).then_inc(S["pj_hi"], 1)
                gi = 0

                def exp_tile(n):
                    act.wait_ge(S["max_done"], 8 * b + n + 1)
                    act.wait_ge(S["pT_done"], CREDIT + 12 * b + pT_count(n - 1))
                    act.wait_ge(S["yrow_done"], CREDIT + 8 * b + max(n - 2, 0))
                    keys = (n + 1) * P
                    s = ps_h[:, 2 * (n % 2):2 * (n % 2) + 2, :].rearrange("p a c -> p (a c)")[:, 0:keys]
                    act.activation(probs[:, n % 2, 0:keys], s, ACT.Exp, bias=neg_max[:, n:n + 1], scale=SCALE,
                                   accum_out=row_sum[:, n:n + 1]).then_inc(S["exp_done"], 1)

                def pT_high(n):
                    for c in range(n // 4 + 1):
                        g = pT_count(n) + c
                        w = min(4, n + 1 - 4 * c) * P
                        act.wait_ge(S["pT_done"], CREDIT + 12 * b + g + 1)
                        act.wait_ge(S["pv_done"], CREDIT + 8 * b + (pv_before(g - 2) if g >= 2 else 0))
                        act.activation(pT_h[:, g % 2, 0:w], ps_p[g % 2][:, 0:w], ACT.Copy)\
                            .then_inc(S["ph_done"], 1)

                def finish(j):
                    act.wait_ge(S["yt_done"], CREDIT + 2 * b + j + 1)
                    act.wait_ge(S["fc_done"], CREDIT + 2 * b + j)
                    act.activation(yT_h[:, :], yT[:, :], ACT.Copy).then_inc(S["yh_done"], 1)

                exp_tile(0)
                for n in range(BT):
                    if n + 1 < BT:
                        exp_tile(n + 1)
                    pT_high(n)
                    if n == 5:
                        finish(0)
                finish(1)

            xh(MACROS, 0)
            sigmoids(MACROS)
            ffn_steps(act, 1, step)
            gh(2 * TILES - 1)

        @block.tensor
        def _(pe):
            for name in ("gT_done", "h_done", "y_done", "pj_done", "pv_done", "pT_done", "fc_done", "a_xT", "yT_done"):
                pe.sem_inc(S[name], CREDIT)
            def product(dst, a_h, a_l, b_h, b_l, masked=None):
                pe.matmul(dst, a_h, b_h, start=True, stop=False)
                if masked is not None:
                    pe.matmul(masked, ident_r[:, :], causal_r[:, :], start=False, stop=False)
                pe.matmul(dst, a_h, b_l, start=False, stop=False)
                return pe.matmul(dst, a_l, b_h, start=False, stop=True)

            def transpose_rows(rows, done):
                for t in range(MT):
                    last = pe.transpose(ps_t[:, t * P:(t + 1) * P], rows(t), ident[:, :])
                last.then_inc(done, 1)

            def xT(mg):
                pe.wait_ge(S["xn_done"], mg + 1)
                wait_for(pe, S["xl_done"], mg)
                transpose_rows(lambda t: xn[:, t, :], S["xT_done"])

            def router(mg, parity):
                pe.wait_ge(S["xl_done"], mg + 1)
                wait_for(pe, S["lgc_done"], mg)
                for t in range(MT):
                    ts = slice(t * P, (t + 1) * P)
                    last = product(ps_lg[:, t * E:(t + 1) * E], xT_h[:, parity, ts], xT_l[:, parity, ts],
                                   wg_h[:, :], wg_l[:, :])
                last.then_inc(S["lg_done"], 1)

            def pair(k, tg, q):
                n = 4 * tg + q
                wait_for(pe, S["gated_done"], n - 1)
                s = 2 * (q % 2)
                ts = slice((k % MT) * P, (k % MT + 1) * P)
                a_h, a_l = xT_h[:, (k // MT) % 2, ts], xT_l[:, (k // MT) % 2, ts]
                for e in range(2):
                    pe.matmul(ps_h[:, s + e, :], a_h, w1_h[:, 2 * q + e, :], start=True, stop=False)
                    pe.matmul(ps_h[:, s + e, :], a_h, w1_l[:, 2 * q + e, :], start=False, stop=False)
                for e in range(2):
                    last = pe.matmul(ps_h[:, s + e, :], a_l, w1_h[:, 2 * q + e, :], start=False, stop=True)
                last.then_inc(S["h_done"], 1)

            def gT(k, tg):
                pe.wait_ge(S["gsum_done"], CREDIT + tg + 1)
                wait_for(pe, S["gl_done"], CREDIT + tg)
                for c in range(HC):
                    last = pe.transpose(ps_g[:, c * P:(c + 1) * P], g_sum[:, k % 2, c * P:(c + 1) * P], ident[:, :])
                last.then_inc(S["gT_done"], 1)

            def down(tg):
                pe.wait_ge(S["gl_done"], CREDIT + tg + 1)
                wait_for(pe, S["x_done"], CREDIT + tg)
                for c in range(HC):
                    cs = slice(c * P, (c + 1) * P)
                    pe.matmul(ps_y[:, 0:D], gT_h[:, cs], wo_h[:, c, :], start=c == 0, stop=False)
                    pe.matmul(ps_y[:, 0:D], gT_h[:, cs], wo_l[:, c, :], start=False, stop=False)
                    last = pe.matmul(ps_y[:, 0:D], gT_l[:, cs], wo_h[:, c, :], start=False, stop=c == HC - 1)
                last.then_inc(S["y_done"], 1)

            def step(k, tg, mg, nxt):
                for q in range(4):
                    pair(k, tg, q)
                    if nxt is not None and q == 1:
                        if k in (2, 5):
                            xT(mg + 1)
                        if k in (3, 6):
                            router(mg + 1, (k // MT + 1) % 2)
                    if q == 2 and k > 0:
                        gT(k - 1, tg - 1)
                if k > 0:
                    down(tg - 1)

            pe.wait_ge(S["const_id"], 4)
            xT(0)
            pe.wait_ge(S["b1_in"], 16)
            pe.transpose(ps_g[:, 0:E * MT], b1_rows[:, :], ident[0:E * MT, 0:E * MT]).then_inc(S["b1_t"], 1)
            for e in range(E):
                pe.wait_ge(S["w1_sub"], e // (E // 2) + 1)
                pe.wait_ge(S["b1_put"], 1)
                if e >= 4:
                    pe.wait_ge(S["w_lo"], e - 3)
                for j in range(MT):
                    last = pe.transpose(ps_h[:, e % 4, j * P:(j + 1) * P], w1_rows[:, e * MT + j, :], ident[:, :])
                last.then_inc(S["w_tp"], 1)
            pe.wait_ge(S["wprep"], 2)
            pe.transpose(ps_lg[:, 0:E], wg_rows[:, :], ident[0:E, 0:E]).then_inc(S["w_tp"], 1)
            pe.wait_ge(S["small_in"], 32)
            for c in range(HC):
                last = pe.transpose(ps_y[:, c * D:(c + 1) * D], wo_rows[:, c * P:(c + 1) * P], ident[:, :])
            last.then_inc(S["w_tp"], 1)
            pe.wait_ge(S["w_lo"], E + 2)
            router(0, 0)
            ffn_steps(pe, 0, step)
            gT(7, TILES - 1)
            down(TILES - 1)

            pe.wait_ge(S["comb_done"], MACROS)
            pe.wait_ge(S["x_done"], CREDIT + TILES)
            pe.wait_ge(S["sq_hi"], 3)
            pe.wait_ge(S["sq_lo"], 1)
            with pe.Fori(0, B) as b:
                for j in range(2):
                    pe.wait_ge(S["a_xn"], CREDIT + 2 * b + j + 1)
                    pe.wait_ge(S["a_xl"], CREDIT + 2 * b + j)
                    if j == 0:
                        pe.wait_ge(S["yt_done"], CREDIT + 2 * b)
                    transpose_rows(lambda t: xn_full[:, t, :], S["a_xT"])
                for j in range(2):
                    pe.wait_ge(S["a_xl"], CREDIT + 2 * b + j + 1)
                    for c in range(3):
                        u = 3 * j + c
                        pe.wait_ge(S["exp_done"], CREDIT + 8 * b)
                        if u >= 4:
                            pe.wait_ge(S["pj_lo"], 6 * b + u - 3)
                        bank = ps_h[:, u % 4, :]
                        if c < 2:
                            last = product(bank, sq_h[:, c, :], sq_l[:, c, :], xT_h[:, j, :], xT_l[:, j, :])
                        else:
                            for t in range(MT):
                                ts = slice(t * P, (t + 1) * P)
                                last = product(bank[:, ts], xT_h[:, j, ts], xT_l[:, j, ts], sq_h[:, 2, :], sq_l[:, 2, :])
                        last.then_inc(S["pj_done"], 1)

                def scores(n):
                    if n < 2:
                        pe.wait_ge(S["pj_lo"], 6 * b + 6)
                    else:
                        pe.wait_ge(S["exp_done"], CREDIT + 8 * b + n - 1)
                    ns = slice(n * P, (n + 1) * P)
                    for c in range(n // 4 + 1):
                        w = min(4, n + 1 - 4 * c) * P
                        ks = slice(c * 512, c * 512 + w)
                        bank = ps_h[:, 2 * (n % 2) + c, :]
                        diag = c == n // 4
                        last = product(bank[:, 0:w], q_h[:, ns], q_l[:, ns], k_h[:, ks], k_l[:, ks],
                                       bank[:, w - P:w] if diag else None)
                    last.then_inc(S["sc_done"], 1)

                def probs_T(n):
                    pe.wait_ge(S["exp_done"], CREDIT + 8 * b + n + 1)
                    for c in range(n // 4 + 1):
                        g = pT_count(n) + c
                        pe.wait_ge(S["pl_done"], CREDIT + 12 * b + max(g - 1, 0))
                        for kb in range(4 * c, min(4 * c + 4, n + 1)):
                            o = (kb - 4 * c) * P
                            last = pe.transpose(ps_p[g % 2][:, o:o + P], probs[:, n % 2, kb * P:(kb + 1) * P],
                                                ident[:, :])
                        last.then_inc(S["pT_done"], 1)

                def pv(n):
                    pe.wait_ge(S["yrow_done"], CREDIT + 8 * b + n)
                    pe.wait_ge(S["xa_done"], CREDIT + 2 * b + n // 6)
                    for kb in range(n + 1):
                        c = kb // 4
                        g = pT_count(n) + c
                        if kb % 4 == 0:
                            pe.wait_ge(S["pl_done"], CREDIT + 12 * b + g + 1)
                        o = (kb % 4) * P
                        a_h, a_l = pT_h[:, g % 2, o:o + P], pT_l[:, g % 2, o:o + P]
                        pe.matmul(ps_y[:, 0:D], a_h, v_h[:, kb, :], start=kb == 0, stop=False)
                        pe.matmul(ps_y[:, 0:D], a_h, v_l[:, kb, :], start=False, stop=False)
                        last = pe.matmul(ps_y[:, 0:D], a_l, v_h[:, kb, :], start=False, stop=kb == n)
                    last.then_inc(S["pv_done"], 1)

                def finish_T(j):
                    pe.wait_ge(S["yn_done"], CREDIT + 2 * b + j + 1)
                    pe.wait_ge(S["a_xl"], CREDIT + 2 * b + 2)
                    pe.wait_ge(S["yt_done"], CREDIT + 2 * b + j)
                    transpose_rows(lambda t: yn[:, t, :], S["yT_done"])

                def finish_fc(j):
                    pe.wait_ge(S["yl_done"], 2 * b + j + 1)
                    pe.wait_ge(S["yrow_done"], CREDIT + 8 * b + (6 if j == 0 else 8))
                    for t in range(MT):
                        ts = slice(t * P, (t + 1) * P)
                        last = product(ps_y[:, ts], yT_h[:, ts], yT_l[:, ts], sq_h[:, 3, :], sq_l[:, 3, :])
                    last.then_inc(S["fc_done"], 1)

                scores(0)
                for n in range(BT):
                    if n + 1 < BT:
                        scores(n + 1)
                    probs_T(n)
                    pv(n)
                    if n == 4:
                        finish_T(0)
                    if n == 5:
                        finish_fc(0)
                finish_T(1)
                finish_fc(1)

            pe.wait_ge(S["xa_done"], CREDIT + 2 * B)
            xT(MACROS)
            router(MACROS, 0)
            ffn_steps(pe, 1, step)
            gT(7, 2 * TILES - 1)
            down(2 * TILES - 1)

        @block.vector
        def _(dve):
            chain = Chain(dve, S["dve_chain"])
            for name in ("gl_done", "x_done", "a_xn", "yrow_done", "yt_done", "a_xl", "pl_done", "xa_done", "yn_done"):
                dve.sem_inc(S[name], CREDIT)

            def low(dst, src, high, done):
                dve.tensor_tensor(dst, src, high.bitcast(F32), ALU.subtract).then_inc(done, 1)

            def statistics(mg, tile0):
                dve_stats(dve, chain, lambda t: x[:, tile0 + t, :] if isinstance(tile0, int)
                          else x[:, bass.ds(tile0 + t, 1), :], stats, mean_var, S["stat_done"])

            def normalise(mg, tile0):
                dve.wait_ge(S["rstd_done"], mg + 1)
                wait_for(dve, S["xT_done"], mg)
                for t in range(MT):
                    src = x[:, tile0 + t, 0:D - 1] if isinstance(tile0, int) else x[:, bass.ds(tile0 + t, 1), 0:D - 1]
                    dst = xn[:, t, 0:D - 1] if isinstance(tile0, int) else xn[:, t:t + 1, 0:D - 1]
                    last = dve.tensor_scalar(dst, src, mean_var[:, t, 0:1], rstd[:, t:t + 1],
                                             ALU.subtract, ALU.mult)
                last.then_inc(S["xn_done"], 1)

            def x_low(mg, parity):
                dve.wait_ge(S["xh_done"], mg + 1)
                low(xT_l[:, parity, :], ps_t[:, :], xT_h[:, parity, :], S["xl_done"])

            def route_logits(mg):
                dve.wait_ge(S["lg_done"], mg + 1)
                ins = dve.tensor_copy(logits[:, :, :], ps_lg[:, 0:MT * E].rearrange("p (t e) -> p t e", t=MT))
                for t in range(MT):
                    ins = dve.max(top8[:, t, :], ps_lg[:, t * E:(t + 1) * E])
                ins.then_inc(S["lgc_done"], 1)
                wait_for(dve, S["sig_done"], mg)
                dve.wait_ge(S["lgc_done"], mg + 1)
                dve.tensor_tensor(below_max[:, :, :], logits[:, :, :], top8[:, :, 0:1].to_broadcast([P, MT, E]),
                                  ALU.subtract).then_inc(S["below_done"], 1)
                for t in range(MT):
                    ins = dve.max_index(top_at[:, t, :], top8[:, t, :], logits[:, t, :])
                chain.step(ins)
                chain.wait()
                chain.step(dve.tensor_tensor(is_first[:, :, :], expert_no[:, :, :],
                                             top_at[:, :, 0:1].to_broadcast([P, MT, E]), ALU.is_equal))
                chain.step(dve.tensor_tensor(is_second[:, :, :], expert_no[:, :, :],
                                             top_at[:, :, 1:2].to_broadcast([P, MT, E]), ALU.is_equal))
                chain.wait()
                chain.step(dve.tensor_tensor(is_first[:, :, :], is_first[:, :, :], is_second[:, :, :], ALU.add))

            def route_weights(mg, parity):
                dve.wait_ge(S["sig_done"], mg + 1)
                chain.step(dve.reciprocal(expo[:, :, :], sig_neg[:, :, :]))
                chain.wait()
                chain.step(dve.tensor_tensor(expo[:, :, :], expo[:, :, :], sig_pos[:, :, :], ALU.mult))
                chain.wait()
                chain.step(dve.tensor_reduce(z_all[:, :], expo[:, :, :], AX.X, ALU.add))
                chain.step(dve.tensor_tensor(is_second[:, :, :], expo[:, :, :], is_first[:, :, :], ALU.mult))
                chain.wait()
                chain.step(dve.tensor_reduce(z_top[:, :], is_second[:, :, :], AX.X, ALU.add))
                chain.wait()
                chain.step(dve.scalar_tensor_tensor(out=z_den[:, :], in0=z_all[:, :], scalar=TOPK_EPS,
                                                    in1=z_top[:, :], op0=ALU.mult, op1=ALU.add))
                chain.wait()
                chain.step(dve.reciprocal(z_den[:, :], z_den[:, :]))
                chain.wait()
                dve.scalar_tensor_tensor(out=comb[:, parity, :, :], in0=is_second[:, :, :], scalar=0.5,
                                         in1=z_den[:, :, None].to_broadcast([P, MT, E]), op0=ALU.mult, op1=ALU.mult)
                dve.scalar_tensor_tensor(out=comb_sum[:, parity, :], in0=z_top[:, :], scalar=0.5,
                                         in1=z_den[:, :], op0=ALU.mult, op1=ALU.mult).then_inc(S["comb_done"], 1)

            def pair(k, tg, q):
                dve.wait_ge(S["gate_done"], 4 * tg + q + 1)
                for e in range(2):
                    last = dve.scalar_tensor_tensor(
                        out=gated[:, k % 2, q, e * H:(e + 1) * H], in0=ps_h[:, 2 * (q % 2) + e, 0:H],
                        scalar=comb[:, (k // MT) % 2, k % MT, 2 * q + e:2 * q + e + 1],
                        in1=gate[:, q % 2, e, :], op0=ALU.mult, op1=ALU.mult)
                last.then_inc(S["gated_done"], 1)

            def g_low(tg):
                dve.wait_ge(S["gh_done"], tg + 1)
                low(gT_l[:, :], ps_g[:, 0:HC * P], gT_h[:, :], S["gl_done"])

            def finish(k, tg, tile):
                xt = x[:, tile, :] if isinstance(tile, int) else x[:, bass.ds(tile, 1), :]
                rs = resid[:, k % 2, :] if isinstance(tile, int) else resid[:, k % 2:k % 2 + 1, :]
                br = bo_rows[:, :] if isinstance(tile, int) else bo_rows[:, None, :]
                yr = ps_y[:, 0:D] if isinstance(tile, int) else ps_y[:, None, 0:D]
                chain.step(dve.scalar_tensor_tensor(out=rs, in0=br,
                                                    scalar=comb_sum[:, (k // MT) % 2, k % MT:k % MT + 1],
                                                    in1=xt, op0=ALU.mult, op1=ALU.add))
                chain.wait()
                dve.wait_ge(S["y_done"], CREDIT + tg + 1)
                dve.tensor_tensor(xt, yr, rs, ALU.add).then_inc(S["x_done"], 1)

            def make_step(phase):
                def step(k, tg, mg, nxt):
                    if k in (0, 4, 8):
                        dve.wait_ge(S["comb_done"], mg + 1)
                    wait_for(dve, S["gsum_done"], CREDIT + tg - 1)
                    for q in range(4):
                        pair(k, tg, q)
                        if q == 0 and nxt is not None and k in (1, 4):
                            statistics(mg + 1, nxt * MT)
                        if q == 2 and k > 0:
                            g_low(tg - 1)
                    if k > 0:
                        finish(k - 1, tg - 1, tg - 1 - phase * TILES)
                    if nxt is not None:
                        if k in (1, 4):
                            normalise(mg + 1, nxt * MT)
                        if k in (2, 5):
                            x_low(mg + 1, (k // MT + 1) % 2)
                        if k in (3, 6):
                            route_logits(mg + 1)
                        if k in (3, 7):
                            route_weights(mg + 1, (k // MT + 1) % 2)
                return step

            dve.memset(xn[:, :, D - 1:D], 1.0).then_inc(S["setup_dve"], 1)
            dve.wait_ge(S["x_first"], 16)
            statistics(0, 0)
            dve.wait_ge(S["setup_dve"], 1)
            normalise(0, 0)
            dve.wait_ge(S["b1_t"], 1)
            dve.wait_ge(S["w1_sub"], 2)
            dve.tensor_copy(w1_rows[:, :, D - 1], ps_g[:, 0:E * MT]).then_inc(S["b1_put"], 1)
            x_low(0, 0)
            dve.wait_ge(S["small_in"], 32)
            dve.tensor_scalar(wg_rows[:, 0:D - 1], wg_rows[:, 0:D - 1], wg_rows[:, D - 1:D], None, ALU.subtract)\
                .then_inc(S["wprep"], 1)
            dve.wait_ge(S["wprep"], 1)
            dve.memset(wg_rows[:, D - 1:D], 0.0).then_inc(S["wprep"], 1)
            for e in range(E):
                dve.wait_ge(S["w_hi"], e + 1)
                low(w1_l[:, e, :], ps_h[:, e % 4, :], w1_h[:, e, :], S["w_lo"])
            dve.wait_ge(S["w_hi"], E + 1)
            low(wg_l[:, :], ps_lg[:, 0:E], wg_h[:, :], S["w_lo"])
            dve.wait_ge(S["w_hi"], E + 2)
            low(wo_l[:, :, :], ps_y[:, 0:HC * D].rearrange("p (c d) -> p c d", c=HC), wo_h[:, :, :], S["w_lo"])
            dve.wait_ge(S["sq_hi"], 1)
            low(sq_l[:, :, :], sq_raw[:, :, :], sq_h[:, :, :], S["sq_lo"])
            dve.wait_ge(S["iota_done"], E)
            route_logits(0)
            route_weights(0, 0)
            dve.wait_ge(S["rows_in"], 64)
            dve.wait_ge(S["x_rest"], 16)
            ffn_steps(dve, 0, make_step(0), chain)
            g_low(TILES - 1)
            finish(7, TILES - 1, TILES - 1)

            at_start = chain.n
            PER = 32
            dve.wait_ge(S["x_done"], CREDIT + TILES)
            with dve.Fori(0, B) as b:
                chain.base, chain.n = at_start + b * PER, 0
                for j in range(2):
                    dve_stats(dve, chain, lambda t: x[:, bass.ds(b * BT + j * MT + t, 1), :], stats, mean_var,
                              S["a_stat"])
                    dve.wait_ge(S["a_rstd"], 2 * b + j + 1)
                    dve.wait_ge(S["a_xT"], CREDIT + 2 * b + j)
                    for t in range(MT):
                        last = dve.tensor_scalar(xn_full[:, t:t + 1, :], x[:, bass.ds(b * BT + j * MT + t, 1), :],
                                                 mean_var[:, t, 0:1], rstd[:, t:t + 1], ALU.subtract, ALU.mult)
                    last.then_inc(S["a_xn"], 1)
                    dve.wait_ge(S["a_xh"], 2 * b + j + 1)
                    low(xT_l[:, j, :], ps_t[:, :], xT_h[:, j, :], S["a_xl"])
                for j in range(2):
                    for c, (hi, lo) in enumerate(((q_h, q_l), (k_h, k_l), (v_h, v_l))):
                        u = 3 * j + c
                        dve.wait_ge(S["pj_hi"], 6 * b + u + 1)
                        if c < 2:
                            h, l = hi[:, j * 512:(j + 1) * 512], lo[:, j * 512:(j + 1) * 512]
                        else:
                            h, l = (w[:, j * MT:(j + 1) * MT, :].rearrange("p t d -> p (t d)") for w in (hi, lo))
                        low(l, ps_h[:, u % 4, :], h, S["pj_lo"])

                def maximum(n):
                    dve.wait_ge(S["sc_done"], 8 * b + n + 1)
                    keys = (n + 1) * P
                    s = ps_h[:, 2 * (n % 2):2 * (n % 2) + 2, :].rearrange("p a c -> p (a c)")[:, 0:keys]
                    chain.step(dve.tensor_reduce(row_max[:, n:n + 1], s, AX.X, ALU.max))
                    chain.wait()
                    dve.tensor_scalar(neg_max[:, n:n + 1], row_max[:, n:n + 1], -SCALE, None, ALU.mult)\
                        .then_inc(S["max_done"], 1)

                def pT_low(n):
                    for c in range(n // 4 + 1):
                        g = pT_count(n) + c
                        w = min(4, n + 1 - 4 * c) * P
                        dve.wait_ge(S["ph_done"], 12 * b + g + 1)
                        low(pT_l[:, g % 2, 0:w], ps_p[g % 2][:, 0:w], pT_h[:, g % 2, 0:w], S["pl_done"])

                def rows(n):
                    dve.wait_ge(S["exp_done"], CREDIT + 8 * b + n + 1)
                    chain.step(dve.reciprocal(row_inv[:, n:n + 1], row_sum[:, n:n + 1]))
                    chain.wait()
                    dve.wait_ge(S["pv_done"], CREDIT + 8 * b + n + 1)
                    dve.wait_ge(S["vf_done"], CREDIT + 2 * b + 2)
                    dve.scalar_tensor_tensor(out=y[:, n % MT, :], in0=ps_y[:, 0:D], scalar=row_inv[:, n:n + 1],
                                             in1=v_f[:, n, :], op0=ALU.mult, op1=ALU.add)\
                        .then_inc(S["yrow_done"], 1)

                def finish_norm(j):
                    dve.wait_ge(S["yrow_done"], CREDIT + 8 * b + MT * (j + 1))
                    dve_stats(dve, chain, lambda t: y[:, t, :], y_stats, y_mean_var, S["y_stat"])
                    dve.wait_ge(S["y_rs"], 2 * b + j + 1)
                    dve.wait_ge(S["yT_done"], CREDIT + 2 * b + j)
                    for t in range(MT):
                        last = dve.tensor_scalar(yn[:, t, :], y[:, t, :], y_mean_var[:, t, 0:1], y_rstd[:, t:t + 1],
                                                 ALU.subtract, ALU.mult)
                    last.then_inc(S["yn_done"], 1)

                def finish_split(j):
                    dve.wait_ge(S["yT_done"], CREDIT + 2 * b + j + 1)
                    dve.wait_ge(S["yh_done"], CREDIT + 2 * b + j)
                    dve.tensor_scalar(yT[:, :], ps_t[:, :], gamma_col[:, :], beta_col[:, :], ALU.mult, ALU.add)\
                        .then_inc(S["yt_done"], 1)

                def finish_low(j):
                    dve.wait_ge(S["yt_done"], CREDIT + 2 * b + j + 1)
                    dve.wait_ge(S["yh_done"], CREDIT + 2 * b + j + 1)
                    low(yT_l[:, :], yT[:, :], yT_h[:, :], S["yl_done"])

                def finish_x(j):
                    dve.wait_ge(S["fc_done"], CREDIT + 2 * b + j + 1)
                    dve.wait_ge(S["xb_done"], 2 * b + j + 1)
                    dve.tensor_tensor(x[:, bass.ds(b * BT + j * MT, MT), :],
                                      ps_y[:, :].rearrange("p (t d) -> p t d", t=MT), x_bfc[:, :, :], ALU.add)\
                        .then_inc(S["xa_done"], 1)

                maximum(0)
                for n in range(BT):
                    if n + 1 < BT:
                        maximum(n + 1)
                    pT_low(n)
                    if n == 5:
                        finish_low(0)
                    rows(n)
                    if n == 3:
                        finish_norm(0)
                    if n == 4:
                        finish_split(0)
                    if n == 5:
                        finish_x(0)
                finish_norm(1)
                finish_split(1)
                finish_low(1)
                finish_x(1)
                assert chain.n == PER, chain.n
            chain.base, chain.n = 0, at_start + B * PER

            dve.wait_ge(S["xa_done"], CREDIT + 2 * B)
            statistics(MACROS, 0)
            normalise(MACROS, 0)
            x_low(MACROS, 0)
            route_logits(MACROS)
            route_weights(MACROS, 0)
            ffn_steps(dve, 1, make_step(1), chain)
            g_low(2 * TILES - 1)
            finish(7, 2 * TILES - 1, TILES - 1)


_INS = ["L0_attn_x", "L0_attn_Wq", "L0_attn_Wk", "L0_attn_Wv", "L0_attn_Wfc", "L0_attn_bfc", "L0_attn_gamma",
        "L0_attn_beta", "L0_ffn_Wg", "L0_ffn_W1", "L0_ffn_b1", "L0_ffn_Wo", "L0_ffn_bo"]


def kernel(**inputs):
    import numpy as _np
    import concourse.bacc as _bacc
    from concourse import mybir as _mybir
    from concourse.bass_utils import run_bass_kernel_spmd as _run

    nc = _bacc.Bacc("TRN2", target_bir_lowering=False, num_devices=1)
    arrays, args = {}, []
    for name in _INS:
        a = _np.ascontiguousarray(inputs[name])
        arrays[f"in_{name}_dram"] = a
        args.append(nc.dram_tensor(f"in_{name}_dram", a.shape, _mybir.dt.from_np(a.dtype), kind="ExternalInput").ap())
    shape = inputs["L0_attn_x"].shape
    args.append(nc.dram_tensor("out_0_dram", shape, _mybir.dt.float32, kind="ExternalOutput").ap())
    macaron_kernel(nc, *args)
    r = _run(nc, [arrays], core_ids=[0])
    return r.results[0]["out_0_dram"]
```

```python
from contextlib import ExitStack

import concourse.bass as bass
from concourse import mybir

F32 = mybir.dt.float32
F32R = mybir.dt.float32r
U32 = mybir.dt.uint32
ALU = mybir.AluOpType
ACT = mybir.ActivationFunctionType
AX = mybir.AxisListType

P = 128
LN_EPS = 1e-05
TOPK_EPS = 1e-09
MASKED = -1e30
RING = 4
CREDIT = 1


class Chain:

    def __init__(self, eng, sem):
        self.eng, self.sem, self.base, self.n = eng, sem, 0, 0

    def step(self, ins):
        ins.then_inc(self.sem, 1)
        self.n += 1

    def wait(self):
        self.eng.wait_ge(self.sem, self.base + self.n)


def wait_for(eng, sem, count):
    if not (isinstance(count, int) and count <= 0):
        eng.wait_ge(sem, count)


def pT_count(n):
    return sum(t // 4 + 1 for t in range(max(n, 0)))


def pv_before(g):
    n = 0
    while pT_count(n + 1) <= g:
        n += 1
    return n + 1


SIDE = {(4, 0): ("xT", 0), (5, 0): ("q", 0), (5, 1): ("k", 0), (6, 0): ("xT", 1), (6, 1): ("yT", 0),
        (7, 0): ("v", 0), (7, 1): ("fc", 0), (8, 0): ("q", 1), (8, 2): ("k", 1), (9, 2): ("v", 1),
        (10, 1): ("yT", 1), (11, 1): ("fc", 1)}
PROJECTIONS = [("q", 0), ("k", 0), ("v", 0), ("q", 1), ("k", 1), ("v", 1)]
FIRST_UNITS = [("xT", 0), ("xT", 1)] + PROJECTIONS
OWN = ("yT", "fc")
AHEAD = 4


def macaron_kernel(nc, x_in, wq, wk, wv, wfc, bfc, gamma, beta, wg, w1, b1, wo, bo, out):
    B, N, D = x_in.shape
    E, H2, _ = w1.shape
    H = H2 // 2
    HC = H // P
    TILES = B * N // P
    MT = 4
    MACROS = TILES // MT
    BT = N // P
    SCALE = 1.0 / float(D) ** 0.5
    assert D == P and H2 == 512 and E == 8 and BT == 2 * MT

    x_tiles = x_in.rearrange("b (t p) d -> p (b t) d", p=P)
    out_tiles = out.rearrange("b (t p) d -> p (b t) d", p=P)

    with ExitStack() as ctx:
        def sb(name, shape, dt=F32):
            return ctx.enter_context(nc.sbuf_tensor(name, shape, dt))

        def ps(name, shape):
            return ctx.enter_context(nc.psum_tensor(name, shape, F32))

        def sem(name):
            return ctx.enter_context(nc.semaphore(name))

        x = sb("x", [P, TILES, D])
        ident = sb("ident", [P, P])
        ident_r = sb("ident_r", [P, P], F32R)
        causal_f = sb("causal_f", [P, P])
        causal_r = sb("causal_r", [P, P], F32R)
        expert_no = sb("expert_no", [P, MT, E])
        minus_half = sb("minus_half", [P, TILES])
        ln_eps = sb("ln_eps", [P, TILES])
        bo_rows = sb("bo_rows", [P, D])
        bfc_rows = sb("bfc_rows", [P, D])
        gamma_col = sb("gamma_col", [P, 1])
        beta_col = sb("beta_col", [P, 1])
        last_col = sb("last_col", [P, E * MT])
        w1_rows = sb("w1_rows", [P, E * MT, D])
        b1_rows = sb("b1_rows", [E * MT, P])
        wg_rows = sb("wg_rows", [E, D])
        wo_rows = sb("wo_rows", [D, H])
        sq_raw = sb("sq_raw", [P, 4, D])
        w1_h = sb("w1_h", [P, E, H2], F32R)
        w1_l = sb("w1_l", [P, E, H2], F32R)
        wg_h = sb("wg_h", [P, E], F32R)
        wg_l = sb("wg_l", [P, E], F32R)
        wo_h = sb("wo_h", [P, HC, D], F32R)
        wo_l = sb("wo_l", [P, HC, D], F32R)
        sq_h = sb("sq_h", [P, 4, D], F32R)
        sq_l = sb("sq_l", [P, 4, D], F32R)
        stats = sb("stats", [P, MT, 6])
        wait_carrier = sb("wait_carrier", [P, 1])
        mean_var = sb("mean_var", [P, MT, 2])
        var_eps = sb("var_eps", [P, MT])
        rstd = sb("rstd", [P, MT])
        xn = sb("xn", [P, MT, D])
        xn_half = sb("xn_half", [P, 2, MT, D])
        b_stats = sb("b_stats", [P, TILES, 6])
        b_mean_var = sb("b_mean_var", [P, TILES, 2])
        b_var_eps = sb("b_var_eps", [P, TILES])
        b_rstd = sb("b_rstd", [P, TILES])
        xT_h = sb("xT_h", [P, 2, MT * P], F32R)
        xT_l = sb("xT_l", [P, 2, MT * P], F32R)
        logits = sb("logits", [P, MT, E])
        top8 = sb("top8", [P, MT, 8])
        top_at = sb("top_at", [P, MT, 8], U32)
        below_max = sb("below_max", [P, MT, E])
        sig_pos = sb("sig_pos", [P, MT, E])
        sig_neg = sb("sig_neg", [P, MT, E])
        expo = sb("expo", [P, MT, E])
        is_first = sb("is_first", [P, MT, E])
        is_second = sb("is_second", [P, MT, E])
        chosen = sb("chosen", [P, MT, E])
        exp_all = sb("exp_all", [P, MT, E])
        exp_top = sb("exp_top", [P, MT, E])
        z_inv = sb("z_inv", [P, MT])
        z_all = sb("z_all", [P, MT])
        z_top = sb("z_top", [P, MT])
        z_den = sb("z_den", [P, MT])
        comb = sb("comb", [P, 2, MT, E])
        comb_sum = sb("comb_sum", [P, 2, MT])
        gate = sb("gate", [P, RING, H])
        gated = sb("gated", [P, 2, E, H])
        g_sum = sb("g_sum", [P, 2, H])
        gT_h = sb("gT_h", [P, HC * P], F32R)
        gT_l = sb("gT_l", [P, HC * P], F32R)
        bo_comb = sb("bo_comb", [P, MT, D])
        resid = sb("resid", [P, 2, MT, D])
        q_h = sb("q_h", [P, N], F32R)
        q_l = sb("q_l", [P, N], F32R)
        k_h = sb("k_h", [P, 2 * N], F32R)
        k_l = sb("k_l", [P, 2 * N], F32R)
        v_h = sb("v_h", [P, 2 * BT * D], F32R)
        v_l = sb("v_l", [P, 2 * BT * D], F32R)
        v_f = sb("v_f", [P, 2 * BT * D])
        row_max = sb("row_max", [P, BT])
        neg_max = sb("neg_max", [P, BT])
        row_sum = sb("row_sum", [P, BT])
        row_inv = sb("row_inv", [P, BT])
        probs = w1_rows[:, 0:2 * BT, :].rearrange("p (a t) d -> p a (t d)", a=2)
        pT_h = sb("pT_h", [P, 4, MT * P], F32R)
        pT_l = sb("pT_l", [P, 4, MT * P], F32R)
        y = w1_rows[:, 2 * BT:3 * BT, :]
        y_stats = sb("y_stats", [P, MT, 6])
        y_mean_var = sb("y_mean_var", [P, MT, 2])
        y_var_eps = sb("y_var_eps", [P, MT])
        y_rstd = sb("y_rstd", [P, MT])
        yn = sb("yn", [P, MT, D])
        yT = sb("yT", [P, MT * P])
        yT_h = sb("yT_h", [P, MT * P], F32R)
        yT_l = sb("yT_l", [P, MT * P], F32R)
        x_bfc = sb("x_bfc", [P, MT, D])

        ps_h = ps("ps_h", [P, RING, 512])
        ps_t = ps("ps_t", [P, 512])
        ps_lg = ps("ps_lg", [P, 512])
        ps_g = ps("ps_g", [P, 512])
        ps_y = ps("ps_y", [P, 512])
        ps_p = [ps_lg, ps_g]
        first_banks = [t[:, :] for t in (ps_t, ps_lg)] + [ps_h[:, 0, :], ps_h[:, 1, :], ps_g[:, :],
                                                          ps_h[:, 2, :], ps_h[:, 3, :], ps_y[:, :]]

        names = """x_first x_rest w1_in0 w1_in1 w1_in2 w1_in3 b1_in small_in sq_in rows_in const_id const_ones
            wprep last_col w1_sub_pool w1_sub_dve w_tp w_hi w_lo wg_tp wg_hi wg_lo wo_tp wo_hi wo_lo b1_t b1_put sq_hi sq_lo setup_dve
            stat_done rstd_done xn_done xT_done xh_done xl_done lg_done lgc_done below_done sig_done comb_done
            bo_done resid_done h_done gate_done gated_done gsum_done gT_done gh_done gl_done y_done x_done
            x_stat a_stat a_rstd a_xn a_xT a_xh a_xl pj_done pj_hi pj_lo vf_done sc_done max_done exp_done
            pT_done ph_done pl_done pv_done yrow_done y_stat y_rs yn_done yT_done yt_done yh_done yl_done
            fc_done xb_done xa_done out_done dve_chain pool_chain""".split()
        S = {n: sem(n) for n in names}
        block = ctx.enter_context(nc.Block())

        @block.sync
        def _(sp):
            w1_blocks = w1.rearrange("e (j p) d -> p (e j) d", p=P)
            sp.dma_start(x[:, 0:MT, :], x_tiles[:, 0:MT, :]).then_inc(S["x_first"], 16)
            for c in range(4):
                cs = slice(c * 2 * MT, (c + 1) * 2 * MT)
                sp.dma_start(w1_rows[:, cs, :], w1_blocks[:, cs, :]).then_inc(S[f"w1_in{c}"], 16)
            sp.dma_start(x[:, MT:TILES, :], x_tiles[:, MT:TILES, :]).then_inc(S["x_rest"], 16)
            for m in range(MACROS):
                sp.wait_ge(S["x_done"], CREDIT + TILES + MT * (m + 1))
                sp.dma_start(out_tiles[:, m * MT:(m + 1) * MT, :], x[:, m * MT:(m + 1) * MT, :])\
                    .then_inc(S["out_done"], 16)
            sp.wait_ge(S["out_done"], 16 * MACROS)

        def pool_rstd(pool, chain, var, eps_out, result, done):
            n = var.shape[1]
            chain.step(pool.tensor_tensor(eps_out, var, ln_eps[:, 0:n], ALU.add))
            chain.wait()
            pool.tensor_tensor(result, eps_out, minus_half[:, 0:n], ALU.pow).then_inc(done, 1)

        def ffn_steps(phase, step, chain, loop):
            t0 = phase * TILES
            m0 = phase * MACROS
            passes = TILES // 8 - 1
            for k in range(2):
                step(k, t0 + k, m0, 1)
            start = chain.n if chain else 0
            with loop(0, passes) as i:
                if chain:
                    per = chain_per_loop[chain.sem.name]
                    chain.base, chain.n = start + i * per, 0
                for k in range(2, 10):
                    step(k, t0 + i * 8 + k, m0 + i * 2 + k // MT, i * 2 + (k // MT + 1))
                if chain:
                    assert chain.n == per, (chain.sem.name, chain.n)
            if chain:
                chain.base, chain.n = 0, start + passes * per
            for k in range(2, 8):
                m = passes * 2 + k // MT
                step(k, t0 + passes * 8 + k, m0 + m, m + 1 if k < MT else None)

        def attention_steps(step, chain, loop):
            for n in range(AHEAD):
                step(n + BT, -1, True)
            start = chain.n if chain else 0
            with loop(0, B - 1) as b:
                if chain:
                    per = chain_per_attention[chain.sem.name]
                    chain.base, chain.n = start + b * per, 0
                for n in range(AHEAD, AHEAD + BT):
                    step(n, b, True)
                if chain:
                    assert chain.n == per, (chain.sem.name, chain.n)
            if chain:
                chain.base, chain.n = 0, start + (B - 1) * per
            for n in range(AHEAD, BT):
                step(n, B - 1, False)

        chain_per_loop = {"dve_chain": 2 * 15, "pool_chain": 8 * 3 + 2}
        chain_per_attention = {"dve_chain": 8 + 8 + 8, "pool_chain": 2 + 2}

        def at(n, b):
            return (b + 1, n - BT) if n >= BT else (b, n)

        def begun(b):
            return not (isinstance(b, int) and b < 0)

        def slot(b, size):
            return (b % 2) * size

        def side_unit(n, b, more, place):
            u = SIDE.get((n, place))
            if u and begun(b) and (more or u[0] in OWN):
                return u, (b if u[0] in OWN else b + 1)
            return None

        def part(t, lo, n):
            return t[:, lo:lo + n] if isinstance(lo, int) else t[:, bass.ds(lo, n)]

        @block.gpsimd
        def _(pool):
            chain = Chain(pool, S["pool_chain"])
            for name in ("gsum_done", "vf_done", "resid_done"):
                pool.sem_inc(S[name], CREDIT)
            pool.dma_start(b1_rows[:, :], b1.rearrange("e (j p) -> (e j) p", p=P)).then_inc(S["b1_in"], 16)
            pool.memset(ident[:, :], 0.0).then_inc(S["const_id"], 1)
            pool.memset(causal_f[:, :], 0.0).then_inc(S["const_id"], 1)
            pool.memset(minus_half[:, :], -0.5).then_inc(S["const_ones"], 1)
            pool.memset(ln_eps[:, :], LN_EPS).then_inc(S["const_ones"], 1)
            pool.wait_ge(S["const_id"], 2)
            pool.affine_select(out=ident[:, :], in_=ident[:, :], compare_op=ALU.not_equal, fill=1.0, base=0,
                               pattern=[[-1, P]], channel_multiplier=1).then_inc(S["const_id"], 1)
            pool.affine_select(out=causal_f[:, :], in_=causal_f[:, :], compare_op=ALU.is_ge, fill=MASKED, base=0,
                               pattern=[[-1, P]], channel_multiplier=1).then_inc(S["const_id"], 1)
            for e in range(E):
                pool.memset(expert_no[:, :, e:e + 1], float(e)).then_inc(S["const_ones"], 1)
            pool.wait_ge(S["const_ones"], 2)

            def prep(mg):
                pool.wait_ge(S["stat_done"], mg + 1)
                wait_for(pool, S["xn_done"], mg)
                pool_rstd(pool, chain, mean_var[:, :, 1], var_eps[:, :], rstd[:, :], S["rstd_done"])

            def residual(k, tg, tile):
                pool.wait_ge(S["bo_done"], tg + 1)
                wait_for(pool, S["x_done"], CREDIT + tg - 2)
                xt = x[:, tile:tile + 1, :] if isinstance(tile, int) else x[:, bass.ds(tile, 1), :]
                t = k % MT
                pool.tensor_tensor(resid[:, (k // MT) % 2, t:t + 1, :], xt, bo_comb[:, t:t + 1, :], ALU.add)\
                    .then_inc(S["resid_done"], 1)

            prep(0)
            for c in (0, 2):
                lo, hi = c * 2 * MT, (c + 1) * 2 * MT
                pool.wait_ge(S["last_col"], c + 1)
                pool.tensor_tensor(w1_rows[:, lo:hi, 0:D - 1], w1_rows[:, lo:hi, 0:D - 1],
                                   last_col[:, lo:hi, None].to_broadcast([P, hi - lo, D - 1]),
                                   ALU.subtract).then_inc(S["w1_sub_pool"], 1)

            def make_step(phase):
                def step(k, tg, mg, nxt):
                    residual(k, tg, tg - phase * TILES)
                    g = gated[:, k % 2]
                    for e in range(2, E, 2):
                        pool.wait_ge(S["gated_done"], E * tg + e + 2)
                        chain.step(pool.tensor_tensor(g[:, 0:2, :], g[:, 0:2, :], g[:, e:e + 2, :], ALU.add))
                        chain.wait()
                    wait_for(pool, S["gT_done"], CREDIT + tg - 1)
                    pool.tensor_tensor(g_sum[:, k % 2, :], g[:, 0, :], g[:, 1, :], ALU.add)\
                        .then_inc(S["gsum_done"], 1)
                    if k % MT == 0 and nxt is not None:
                        prep(mg + 1)
                return step

            ffn_steps(0, make_step(0), chain, pool.Fori)

            pool.wait_ge(S["a_stat"], 1)
            pool_rstd(pool, chain, b_mean_var[:, :, 1], b_var_eps[:, :], b_rstd[:, :], S["a_rstd"])
            pool.wait_ge(S["a_rstd"], 1)
            pool.wait_ge(S["x_done"], CREDIT + TILES)

            def half_norm(b, j):
                wait_for(pool, S["a_xT"], 2 * b + j - 1)
                tile = b * BT + j * MT
                mean, inv = ((t[:, tile:tile + MT] if isinstance(b, int) else t[:, bass.ds(tile, MT)])
                             for t in (b_mean_var[:, :, 0], b_rstd[:, :]))
                rows = x[:, tile:tile + MT, :] if isinstance(b, int) else x[:, bass.ds(tile, MT), :]
                chain.step(pool.tensor_tensor(xn_half[:, j, :, :], rows,
                                              mean[:, :, None].to_broadcast([P, MT, D]), ALU.subtract))
                chain.wait()
                pool.tensor_tensor(xn_half[:, j, :, :], xn_half[:, j, :, :],
                                   inv[:, :, None].to_broadcast([P, MT, D]), ALU.mult).then_inc(S["a_xn"], 1)

            def v_sum(b, j):
                pool.wait_ge(S["pj_lo"], CREDIT + 6 * b + 3 * j + 3)
                pool.wait_ge(S["xa_done"], CREDIT + (2 * b - 2 if not isinstance(b, int) else max(2 * b - 2, 0)))
                lo = slot(b, BT * D) + j * MT * D
                pool.tensor_tensor(part(v_f, lo, MT * D), part(v_h, lo, MT * D).bitcast(F32),
                                   part(v_l, lo, MT * D).bitcast(F32), ALU.add).then_inc(S["vf_done"], 1)

            def add_bfc(b, j):
                wait_for(pool, S["xa_done"], CREDIT + 2 * b + j)
                pool.tensor_tensor(x_bfc[:, :, :], x[:, bass.ds(b * BT + j * MT, MT), :],
                                   bfc_rows[:, None, :].to_broadcast([P, MT, D]), ALU.add)\
                    .then_inc(S["xb_done"], 1)

            def y_rstd_of(b, j):
                pool.wait_ge(S["y_stat"], 2 * b + j + 1)
                wait_for(pool, S["yn_done"], CREDIT + 2 * b + j)
                pool_rstd(pool, chain, y_mean_var[:, :, 1], y_var_eps[:, :], y_rstd[:, :], S["y_rs"])

            def step_a(n, b, more):
                if n == 4 and more:
                    half_norm(b + 1, 0)
                    half_norm(b + 1, 1)
                if n == 4:
                    y_rstd_of(b, 0)
                    add_bfc(b, 0)
                if n == 7 and more:
                    v_sum(b + 1, 0)
                if n == 8 and begun(b):
                    y_rstd_of(b, 1)
                    add_bfc(b, 1)
                if n == 10 and begun(b):
                    v_sum(b + 1, 1)

            half_norm(0, 0)
            half_norm(0, 1)
            v_sum(0, 0)
            v_sum(0, 1)
            attention_steps(step_a, chain, pool.Fori)
            y_rstd_of(B - 1, 1)
            add_bfc(B - 1, 1)

            prep(MACROS)
            ffn_steps(1, make_step(1), chain, pool.Fori)

        @block.scalar
        def _(act):
            for name in ("exp_done", "yh_done"):
                act.sem_inc(S[name], CREDIT)
            act.dma_start(wg_rows[:, :], wg).then_inc(S["small_in"], 16)
            act.dma_start(wo_rows[:, :], wo).then_inc(S["small_in"], 16)
            for n, w in enumerate((wq, wk, wv, wfc)):
                act.dma_start(sq_raw[:, n, :], w).then_inc(S["sq_in"], 16)
            act.dma_start(bo_rows[:, :], bo.rearrange("(a d) -> a d", a=1).to_broadcast([P, D]))\
                .then_inc(S["rows_in"], 16)
            act.dma_start(bfc_rows[:, :], bfc.rearrange("(a d) -> a d", a=1).to_broadcast([P, D]))\
                .then_inc(S["rows_in"], 16)
            act.dma_start(gamma_col[:, :], gamma.rearrange("(p a) -> p a", a=1)).then_inc(S["rows_in"], 16)
            act.dma_start(beta_col[:, :], beta.rearrange("(p a) -> p a", a=1)).then_inc(S["rows_in"], 16)

            def xh(mg, parity):
                act.wait_ge(S["xT_done"], mg + 1)
                if not (isinstance(mg, int) and mg < 2):
                    act.wait_ge(S["h_done"], CREDIT + 4 * E * (mg - 1))
                act.activation(xT_h[:, parity, :], ps_t[:, :], ACT.Copy).then_inc(S["xh_done"], 1)

            def sigmoids(mg):
                act.wait_ge(S["below_done"], mg + 1)
                wait_for(act, S["comb_done"], mg)
                act.activation(sig_pos[:, :, :], below_max[:, :, :], ACT.Sigmoid)
                act.activation(sig_neg[:, :, :], below_max[:, :, :], ACT.Sigmoid, scale=-1.0)\
                    .then_inc(S["sig_done"], 1)

            def bo_part(k, tg, mg):
                if k % MT == 0:
                    act.wait_ge(S["comb_done"], mg + 1)
                wait_for(act, S["resid_done"], CREDIT + tg - 1)
                t = k % MT
                act.activation(bo_comb[:, t, :], bo_rows[:, :], ACT.Copy, scale=comb_sum[:, (k // MT) % 2, t:t + 1])\
                    .then_inc(S["bo_done"], 1)

            def gh(tg):
                act.wait_ge(S["gT_done"], CREDIT + tg + 1)
                wait_for(act, S["y_done"], CREDIT + tg)
                act.activation(gT_h[:, :], ps_g[:, 0:HC * P], ACT.Copy).then_inc(S["gh_done"], 1)

            def step(k, tg, mg, nxt):
                for e in range(E):
                    n = E * tg + e
                    act.wait_ge(S["h_done"], CREDIT + n + 1)
                    wait_for(act, S["gated_done"], n - RING + 1)
                    act.activation(gate[:, e % RING, :], ps_h[:, e % RING, H:2 * H], ACT.Sigmoid)\
                        .then_inc(S["gate_done"], 1)
                    if e == 1:
                        bo_part(k, tg, mg)
                    if e == 6 and k > 0:
                        gh(tg - 1)
                    if nxt is not None:
                        if k % MT == 2 and e == 4:
                            xh(mg + 1, (k // MT + 1) % 2)
                        if k % MT == 3 and e == 4:
                            sigmoids(mg + 1)

            xh(0, 0)
            for e in range(E):
                act.wait_ge(S["w_tp"], e + 1)
                act.activation(w1_h[:, e, :], ps_h[:, e % RING, :], ACT.Copy).then_inc(S["w_hi"], 1)
                if e == 0:
                    act.wait_ge(S["wg_tp"], 1)
                    act.activation(wg_h[:, :], ps_lg[:, 0:E], ACT.Copy).then_inc(S["wg_hi"], 1)
            act.wait_ge(S["wo_tp"], 1)
            act.activation(wo_h[:, :, :], ps_y[:, 0:HC * D].rearrange("p (c d) -> p c d", c=HC), ACT.Copy)\
                .then_inc(S["wo_hi"], 1)
            act.wait_ge(S["sq_in"], 64)
            act.activation(sq_h[:, :, :], sq_raw[:, :, :], ACT.Copy).then_inc(S["sq_hi"], 1)
            act.wait_ge(S["const_id"], 4)
            act.activation(ident_r[:, :], ident[:, :], ACT.Copy).then_inc(S["sq_hi"], 1)
            act.activation(causal_r[:, :], causal_f[:, :], ACT.Copy).then_inc(S["sq_hi"], 1)
            act.wait_ge(S["rows_in"], 64)
            sigmoids(0)
            ffn_steps(0, step, None, act.Fori)
            gh(TILES - 1)

            def side(u, b, bank=ps_t[:, :]):
                what, j = u
                if what == "xT":
                    act.wait_ge(S["a_xT"], 2 * b + j + 1)
                    wait_for(act, S["pj_done"], CREDIT + 6 * b)
                    act.activation(xT_h[:, j, :], bank, ACT.Copy).then_inc(S["a_xh"], 1)
                elif what == "yT":
                    act.wait_ge(S["yT_done"], CREDIT + 2 * b + j + 1)
                    wait_for(act, S["fc_done"], CREDIT + 2 * b + j)
                    act.activation(yT_h[:, :], bank, ACT.Identity, bias=beta_col[:, :], scale=gamma_col[:, :])\
                        .then_inc(S["yh_done"], 1)
                else:
                    u = PROJECTIONS.index((what, j))
                    act.wait_ge(S["pj_done"], CREDIT + 6 * b + u + 1)
                    if what == "q":
                        wait_for(act, S["sc_done"], BT * b - (4 if j == 0 else 0))
                        dst = q_h[:, j * 512:(j + 1) * 512]
                    else:
                        wait_for(act, S["pv_done"], CREDIT + BT * (b - 1))
                        if what == "v":
                            wait_for(act, S["vf_done"], CREDIT + 2 * (b - 1))
                        dst = part(k_h if what == "k" else v_h, slot(b, N) + j * 512, 512)
                    act.activation(dst, bank, ACT.Copy).then_inc(S["pj_hi"], 1)

            def exp_tile(b, i):
                act.wait_ge(S["max_done"], BT * b + i + 1)
                wait_for(act, S["pT_done"], CREDIT + 12 * b + (pT_count(i - 1) if i >= 2 else pT_count(i + 7) - 12))
                wait_for(act, S["yrow_done"], CREDIT + BT * b + (i - BT + 1 if i < AHEAD else 0))
                keys = (i + 1) * P
                s = ps_h[:, 2 * (i % 2):2 * (i % 2) + 2, :].rearrange("p a c -> p (a c)")[:, 0:keys]
                act.activation(probs[:, i % 2, 0:keys], s, ACT.Exp, bias=neg_max[:, i:i + 1], scale=SCALE,
                               accum_out=row_sum[:, i:i + 1]).then_inc(S["exp_done"], 1)

            def pT_high(b, i):
                for c in range(i // 4 + 1):
                    g = pT_count(i) + c
                    w = min(4, i + 1 - 4 * c) * P
                    act.wait_ge(S["pT_done"], CREDIT + 12 * b + g + 1)
                    wait_for(act, S["pv_done"], CREDIT + BT * b + (pv_before(g - 4) if g >= 4 else
                                                                  pv_before(g + 8) - BT))
                    act.activation(pT_h[:, g % 4, 0:w], ps_p[g % 2][:, 0:w], ACT.Copy).then_inc(S["ph_done"], 1)

            def step_a(n, b, more):
                if n + 1 < BT or more:
                    exp_tile(*at(n + 1, b))
                first, *later = (side_unit(n, b, more, place) for place in range(3))
                if first:
                    side(*first)
                pT_high(*at(n, b))
                for unit in later:
                    if unit and unit[0][0] != "fc":
                        side(*unit)

            act.wait_ge(S["h_done"], CREDIT + E * TILES)
            for n, u in enumerate(FIRST_UNITS):
                side(u, 0, first_banks[n])
            exp_tile(0, 0)
            attention_steps(step_a, None, act.Fori)
            side(("yT", 1), B - 1)

            xh(MACROS, 0)
            sigmoids(MACROS)
            ffn_steps(1, step, None, act.Fori)
            gh(2 * TILES - 1)

        @block.tensor
        def _(pe):
            for name in ("gT_done", "h_done", "y_done", "pj_done", "pv_done", "pT_done", "fc_done", "yT_done"):
                pe.sem_inc(S[name], CREDIT)

            def product(dst, a_h, a_l, b_h, b_l, masked=None):
                pe.matmul(dst, a_h, b_h, start=True, stop=False)
                if masked is not None:
                    pe.matmul(masked, ident_r[:, :], causal_r[:, :], start=False, stop=False)
                pe.matmul(dst, a_h, b_l, start=False, stop=False)
                return pe.matmul(dst, a_l, b_h, start=False, stop=True)

            def transpose_rows(rows, done):
                for t in range(MT):
                    last = pe.transpose(ps_t[:, t * P:(t + 1) * P], rows(t), ident[:, :])
                last.then_inc(done, 1)

            def xT(mg):
                pe.wait_ge(S["xn_done"], mg + 1)
                wait_for(pe, S["xl_done"], mg)
                transpose_rows(lambda t: xn[:, t, :], S["xT_done"])

            def router(mg, parity):
                pe.wait_ge(S["xl_done"], mg + 1)
                wait_for(pe, S["lgc_done"], mg)
                for t in range(MT):
                    ts = slice(t * P, (t + 1) * P)
                    last = product(ps_lg[:, t * E:(t + 1) * E], xT_h[:, parity, ts], xT_l[:, parity, ts],
                                   wg_h[:, :], wg_l[:, :])
                last.then_inc(S["lg_done"], 1)

            def gT(k, tg):
                pe.wait_ge(S["gsum_done"], CREDIT + tg + 1)
                wait_for(pe, S["gl_done"], CREDIT + tg)
                for c in range(HC):
                    last = pe.transpose(ps_g[:, c * P:(c + 1) * P], g_sum[:, k % 2, c * P:(c + 1) * P], ident[:, :])
                last.then_inc(S["gT_done"], 1)

            def down(tg):
                pe.wait_ge(S["gl_done"], CREDIT + tg + 1)
                wait_for(pe, S["x_done"], CREDIT + tg)
                for c in range(HC):
                    cs = slice(c * P, (c + 1) * P)
                    pe.matmul(ps_y[:, 0:D], gT_h[:, cs], wo_h[:, c, :], start=c == 0, stop=False)
                    pe.matmul(ps_y[:, 0:D], gT_h[:, cs], wo_l[:, c, :], start=False, stop=False)
                    last = pe.matmul(ps_y[:, 0:D], gT_l[:, cs], wo_h[:, c, :], start=False, stop=c == HC - 1)
                last.then_inc(S["y_done"], 1)

            def step(k, tg, mg, nxt):
                for e in range(E):
                    n = E * tg + e
                    wait_for(pe, S["gated_done"], n - RING + 1)
                    if k == 0 and isinstance(tg, int) and tg == 0:
                        pe.wait_ge(S["w_lo"], min(e + RING + 1, E))
                    ts = slice((k % MT) * P, (k % MT + 1) * P)
                    product(ps_h[:, e % RING, :], xT_h[:, (k // MT) % 2, ts], xT_l[:, (k // MT) % 2, ts],
                            w1_h[:, e, :], w1_l[:, e, :]).then_inc(S["h_done"], 1)
                    if e == 2 and k > 1:
                        down(tg - 2)
                    if nxt is not None:
                        if k % MT == 2 and e == 2:
                            xT(mg + 1)
                        if k % MT == 3 and e == 1:
                            router(mg + 1, (k // MT + 1) % 2)
                    if e == 6 and k > 0:
                        gT(k - 1, tg - 1)

            def last_tiles(phase):
                end = (phase + 1) * TILES
                down(end - 2)
                gT(7, end - 1)
                down(end - 1)

            pe.wait_ge(S["const_id"], 4)
            pe.wait_ge(S["b1_in"], 16)
            pe.transpose(ps_g[:, 0:E * MT], b1_rows[:, :], ident[0:E * MT, 0:E * MT]).then_inc(S["b1_t"], 1)
            xT(0)
            pe.wait_ge(S["wprep"], 2)
            pe.transpose(ps_lg[:, 0:E], wg_rows[:, :], ident[0:E, 0:E]).then_inc(S["wg_tp"], 1)
            for e in range(E):
                pe.wait_ge(S["w1_sub_dve" if e // 2 % 2 else "w1_sub_pool"], e // 4 + 1)
                pe.wait_ge(S["b1_put"], e // 2 + 1)
                if e >= RING:
                    pe.wait_ge(S["w_lo"], e - RING + 1)
                for j in range(MT):
                    last = pe.transpose(ps_h[:, e % RING, j * P:(j + 1) * P], w1_rows[:, e * MT + j, :], ident[:, :])
                last.then_inc(S["w_tp"], 1)
                if e == 1:
                    pe.wait_ge(S["wg_lo"], 1)
                    router(0, 0)
            pe.wait_ge(S["small_in"], 32)
            for c in range(HC):
                last = pe.transpose(ps_y[:, c * D:(c + 1) * D], wo_rows[:, c * P:(c + 1) * P], ident[:, :])
            last.then_inc(S["wo_tp"], 1)
            ffn_steps(0, step, None, pe.Fori)
            last_tiles(0)

            def read_out(u, b):
                what, j = u
                if what == "xT":
                    wait_for(pe, S["a_xl"], 2 * b + j + 1)
                elif what == "yT":
                    pe.wait_ge(S["yt_done"], CREDIT + 2 * b + j + 1)
                elif what == "fc":
                    pe.wait_ge(S["xa_done"], CREDIT + 2 * b + j + 1)
                else:
                    pe.wait_ge(S["pj_lo"], CREDIT + 6 * b + PROJECTIONS.index(u) + 1)

            def bank_free(u, b, more):
                order = [v for v in SIDE.values() if more or v[0] in OWN]
                if u == order[0]:
                    read_out(PROJECTIONS[-1], b)
                    wait_for(pe, S["xa_done"], CREDIT + 2 * b)
                else:
                    before = order[order.index(u) - 1]
                    read_out(before, b if before[0] in OWN else b + 1)

            def side(u, b, bank=ps_t[:, :]):
                what, j = u
                if what in ("xT", "yT"):
                    if what == "xT":
                        pe.wait_ge(S["a_xn"], 2 * b + j + 1)
                        source = xn_half[:, j]
                    else:
                        pe.wait_ge(S["yn_done"], CREDIT + 2 * b + j + 1)
                        source = yn
                    for t in range(MT):
                        last = pe.transpose(bank[:, t * P:(t + 1) * P], source[:, t, :], ident[:, :])
                    last.then_inc(S["a_xT" if what == "xT" else "yT_done"], 1)
                    return
                if what == "fc":
                    pe.wait_ge(S["yl_done"], CREDIT + 2 * b + j + 1)
                    rows_h, rows_l, n, done = yT_h, yT_l, 3, S["fc_done"]
                else:
                    pe.wait_ge(S["a_xl"], 2 * b + j + 1)
                    rows_h, rows_l, n, done = xT_h[:, j, :], xT_l[:, j, :], "qkv".find(what), S["pj_done"]
                if what in ("v", "fc"):
                    for t in range(MT):
                        ts = slice(t * P, (t + 1) * P)
                        last = product(bank[:, ts], rows_h[:, ts], rows_l[:, ts], sq_h[:, n, :], sq_l[:, n, :])
                else:
                    last = product(bank[:, :], sq_h[:, n, :], sq_l[:, n, :], rows_h, rows_l)
                last.then_inc(done, 1)

            def scores(b, i):
                pe.wait_ge(S["pj_lo"], CREDIT + 6 * b + (2 if i < MT else 5))
                wait_for(pe, S["exp_done"], CREDIT + BT * b + i - 1)
                ns = slice(i * P, (i + 1) * P)
                for c in range(i // 4 + 1):
                    w = min(4, i + 1 - 4 * c) * P
                    lo = slot(b, N) + c * 512
                    bank = ps_h[:, 2 * (i % 2) + c, :]
                    last = product(bank[:, 0:w], q_h[:, ns], q_l[:, ns], part(k_h, lo, w), part(k_l, lo, w),
                                   bank[:, w - P:w] if c == i // 4 else None)
                last.then_inc(S["sc_done"], 1)

            def probs_T(b, i):
                pe.wait_ge(S["exp_done"], CREDIT + BT * b + i + 1)
                for c in range(i // 4 + 1):
                    g = pT_count(i) + c
                    wait_for(pe, S["pl_done"], 12 * b + g - 1)
                    for kb in range(4 * c, min(4 * c + 4, i + 1)):
                        o = (kb - 4 * c) * P
                        last = pe.transpose(ps_p[g % 2][:, o:o + P], probs[:, i % 2, kb * P:(kb + 1) * P], ident[:, :])
                    last.then_inc(S["pT_done"], 1)

            def pv(b, i):
                wait_for(pe, S["yrow_done"], CREDIT + BT * b + i)
                pe.wait_ge(S["pj_lo"], CREDIT + 6 * b + (3 if i < MT else 6))
                for kb in range(i + 1):
                    g = pT_count(i) + kb // 4
                    if kb % 4 == 0:
                        pe.wait_ge(S["pl_done"], 12 * b + g + 1)
                    o = (kb % 4) * P
                    a_h, a_l = pT_h[:, g % 4, o:o + P], pT_l[:, g % 4, o:o + P]
                    lo = slot(b, N) + kb * D
                    pe.matmul(ps_y[:, 0:D], a_h, part(v_h, lo, D), start=kb == 0, stop=False)
                    pe.matmul(ps_y[:, 0:D], a_h, part(v_l, lo, D), start=False, stop=False)
                    last = pe.matmul(ps_y[:, 0:D], a_l, part(v_h, lo, D), start=False, stop=kb == i)
                last.then_inc(S["pv_done"], 1)

            def step_a(n, b, more):
                def side_at(place):
                    unit = side_unit(n, b, more, place)
                    if unit:
                        bank_free(unit[0], b, more)
                        side(*unit)
                side_at(0)
                probs_T(*at(n, b))
                if n + 2 < BT or more:
                    scores(*at(n + 2, b))
                side_at(1)
                if (n != BT or begun(b)):
                    pv(*at(n - 1, b))
                side_at(2)

            pe.wait_ge(S["comb_done"], MACROS)
            pe.wait_ge(S["x_done"], CREDIT + TILES)
            pe.wait_ge(S["sq_hi"], 3)
            pe.wait_ge(S["sq_lo"], 1)
            for n, u in enumerate(FIRST_UNITS):
                side(u, 0, first_banks[n])
            scores(0, 0)
            read_out(PROJECTIONS[-1], 0)
            scores(0, 1)
            attention_steps(step_a, None, pe.Fori)
            pv(B - 1, BT - 1)
            for u in (("yT", 1), ("fc", 1)):
                bank_free(u, B - 1, False)
                side(u, B - 1)

            pe.wait_ge(S["xa_done"], CREDIT + 2 * B)
            xT(MACROS)
            router(MACROS, 0)
            ffn_steps(1, step, None, pe.Fori)
            last_tiles(1)

        @block.vector
        def _(dve):
            chain = Chain(dve, S["dve_chain"])
            for name in ("gl_done", "x_done", "yrow_done", "xa_done", "yn_done", "pj_lo", "yt_done", "yl_done"):
                dve.sem_inc(S[name], CREDIT)

            def low(dst, src, high, done):
                dve.tensor_tensor(dst, src, high.bitcast(F32), ALU.subtract).then_inc(done, 1)

            def tile_of_x(t, cols=D):
                return x[:, t:t + 1, 0:cols] if isinstance(t, int) else x[:, bass.ds(t, 1), 0:cols]

            def statistics(tile0, t):
                if t < MT:
                    chain.step(dve.bn_stats(stats[:, t, :], tile_of_x(tile0 + t)))
                    return
                chain.wait()
                dve.tensor_copy(wait_carrier[:, :], stats[:, 0, 0:1])
                for t in range(MT):
                    last = dve.bn_aggr(mean_var[:, t, :], stats[:, t, :])
                last.then_inc(S["stat_done"], 1)

            def normalise(mg, tile0, t):
                if t == 0:
                    dve.wait_ge(S["rstd_done"], mg + 1)
                    wait_for(dve, S["xT_done"], mg)
                ins = dve.tensor_scalar(xn[:, t:t + 1, 0:D - 1], tile_of_x(tile0 + t, D - 1),
                                        mean_var[:, t, 0:1], rstd[:, t:t + 1], ALU.subtract, ALU.mult)
                if t == MT - 1:
                    ins.then_inc(S["xn_done"], 1)

            def x_low(mg, parity, half):
                if half == 0:
                    dve.wait_ge(S["xh_done"], mg + 1)
                cs = slice(half * 2 * P, (half + 1) * 2 * P)
                ins = dve.tensor_tensor(xT_l[:, parity, cs], ps_t[:, cs], xT_h[:, parity, cs].bitcast(F32),
                                        ALU.subtract)
                if half == 1:
                    ins.then_inc(S["xl_done"], 1)

            def route(part_no, mg, parity):
                if part_no == 1:
                    dve.wait_ge(S["lg_done"], mg + 1)
                    dve.tensor_copy(logits[:, :, :], ps_lg[:, 0:MT * E].rearrange("p (t e) -> p t e", t=MT))
                    for t in range(MT):
                        ins = dve.max(top8[:, t, :], ps_lg[:, t * E:(t + 1) * E])
                    ins.then_inc(S["lgc_done"], 1)
                elif part_no == 2:
                    wait_for(dve, S["sig_done"], mg)
                    dve.wait_ge(S["lgc_done"], mg + 1)
                    dve.tensor_tensor(below_max[:, :, :], logits[:, :, :], top8[:, :, 0:1].to_broadcast([P, MT, E]),
                                      ALU.subtract).then_inc(S["below_done"], 1)
                    for t in range(MT):
                        ins = dve.max_index(top_at[:, t, :], top8[:, t, :], logits[:, t, :])
                    chain.step(ins)
                elif part_no == 3:
                    chain.wait()
                    chain.step(dve.tensor_tensor(is_first[:, :, :], expert_no[:, :, :],
                                                 top_at[:, :, 0:1].to_broadcast([P, MT, E]), ALU.is_equal))
                    chain.step(dve.tensor_tensor(is_second[:, :, :], expert_no[:, :, :],
                                                 top_at[:, :, 1:2].to_broadcast([P, MT, E]), ALU.is_equal))
                elif part_no == 4:
                    chain.wait()
                    chain.step(dve.tensor_tensor(chosen[:, :, :], is_first[:, :, :], is_second[:, :, :], ALU.add))
                elif part_no == 5:
                    dve.wait_ge(S["sig_done"], mg + 1)
                    chain.step(dve.reciprocal(expo[:, :, :], sig_neg[:, :, :]))
                elif part_no == 6:
                    chain.wait()
                    chain.step(dve.tensor_tensor(exp_all[:, :, :], expo[:, :, :], sig_pos[:, :, :], ALU.mult))
                elif part_no == 7:
                    chain.wait()
                    chain.step(dve.tensor_reduce(z_all[:, :], exp_all[:, :, :], AX.X, ALU.add))
                    chain.step(dve.tensor_tensor(exp_top[:, :, :], exp_all[:, :, :], chosen[:, :, :], ALU.mult))
                elif part_no == 8:
                    chain.wait()
                    chain.step(dve.tensor_reduce(z_top[:, :], exp_top[:, :, :], AX.X, ALU.add))
                elif part_no == 9:
                    chain.wait()
                    chain.step(dve.scalar_tensor_tensor(out=z_den[:, :], in0=z_all[:, :], scalar=TOPK_EPS,
                                                        in1=z_top[:, :], op0=ALU.mult, op1=ALU.add))
                elif part_no == 10:
                    chain.wait()
                    chain.step(dve.reciprocal(z_inv[:, :], z_den[:, :]))
                elif part_no == 11:
                    chain.wait()
                    dve.scalar_tensor_tensor(out=comb[:, parity, :, :], in0=exp_top[:, :, :], scalar=0.5,
                                             in1=z_inv[:, :, None].to_broadcast([P, MT, E]),
                                             op0=ALU.mult, op1=ALU.mult)
                    dve.scalar_tensor_tensor(out=comb_sum[:, parity, :], in0=z_top[:, :], scalar=0.5,
                                             in1=z_inv[:, :], op0=ALU.mult, op1=ALU.mult)\
                        .then_inc(S["comb_done"], 1)

            def g_low(tg):
                dve.wait_ge(S["gh_done"], tg + 1)
                low(gT_l[:, :], ps_g[:, 0:HC * P], gT_h[:, :], S["gl_done"])

            def finish(k, tg, mg, tile):
                dve.wait_ge(S["y_done"], CREDIT + tg + 1)
                dve.wait_ge(S["resid_done"], CREDIT + tg + 1)
                dve.tensor_tensor(tile_of_x(tile), ps_y[:, None, 0:D],
                                  resid[:, (k // MT) % 2, k % MT:k % MT + 1, :], ALU.add).then_inc(S["x_done"], 1)

            def finished_statistics(tile):
                dve.wait_ge(S["x_done"], CREDIT + tile + 1)
                dst = b_stats[:, tile:tile + 1, :] if isinstance(tile, int) else b_stats[:, bass.ds(tile, 1), :]
                dve.bn_stats(dst, tile_of_x(tile)).then_inc(S["x_stat"], 1)

            def make_step(phase):
                def step(k, tg, mg, nxt):
                    if k % MT == 0:
                        dve.wait_ge(S["comb_done"], mg + 1)
                    wait_for(dve, S["gsum_done"], CREDIT + tg - 1)
                    for e in range(E):
                        dve.wait_ge(S["gate_done"], E * tg + e + 1)
                        dve.scalar_tensor_tensor(
                            out=gated[:, k % 2, e, :], in0=ps_h[:, e % RING, 0:H],
                            scalar=comb[:, (k // MT) % 2, k % MT, e:e + 1],
                            in1=gate[:, e % RING, :], op0=ALU.mult, op1=ALU.mult).then_inc(S["gated_done"], 1)
                        if nxt is not None:
                            parity = (k // MT + 1) % 2
                            if k % MT == 0 and e <= MT:
                                statistics(nxt * MT, e)
                            if k % MT == 1 and e >= MT:
                                normalise(mg + 1, nxt * MT, e - MT)
                            if k % MT == 2 and e >= 6:
                                x_low(mg + 1, parity, e - 6)
                            if k % MT == 3:
                                for part_no in ((), (), (1,), (2,), (3, 4), (), (5, 6, 7), (8, 9, 10, 11))[e]:
                                    route(part_no, mg + 1, parity)
                        if e == 6 and k > 0:
                            g_low(tg - 1)
                        if e == 4 and k > 1:
                            finish(k - 2, tg - 2, mg if k % MT > 1 else mg - 1, tg - 2 - phase * TILES)
                        if e == 5 and k > 1 and phase == 0:
                            finished_statistics(tg - 2)
                return step

            def last_tiles(phase):
                end = (phase + 1) * TILES
                m = (phase + 1) * MACROS - 1
                finish(6, end - 2, m, TILES - 2)
                g_low(end - 1)
                finish(7, end - 1, m, TILES - 1)

            dve.memset(xn[:, :, D - 1:D], 1.0).then_inc(S["setup_dve"], 1)
            dve.wait_ge(S["x_first"], 16)
            for t in range(MT + 1):
                statistics(0, t)
            dve.wait_ge(S["small_in"], 32)
            dve.tensor_scalar(wg_rows[:, 0:D - 1], wg_rows[:, 0:D - 1], wg_rows[:, D - 1:D], None, ALU.subtract)\
                .then_inc(S["wprep"], 1)
            for c in range(4):
                cs = slice(c * 2 * MT, (c + 1) * 2 * MT)
                dve.wait_ge(S[f"w1_in{c}"], 16)
                dve.tensor_copy(last_col[:, cs], w1_rows[:, cs, D - 1]).then_inc(S["last_col"], 1)
                dve.wait_ge(S["last_col"], c + 1)
                if c % 2:
                    dve.tensor_tensor(w1_rows[:, cs, 0:D - 1], w1_rows[:, cs, 0:D - 1],
                                      last_col[:, cs, None].to_broadcast([P, 2 * MT, D - 1]),
                                      ALU.subtract).then_inc(S["w1_sub_dve"], 1)
                if c == 0:
                    dve.wait_ge(S["wprep"], 1)
                    dve.memset(wg_rows[:, D - 1:D], 0.0).then_inc(S["wprep"], 1)
                    dve.wait_ge(S["setup_dve"], 1)
                    for t in range(MT):
                        normalise(0, 0, t)
                    dve.wait_ge(S["b1_t"], 1)
                dve.tensor_copy(w1_rows[:, cs, D - 1], ps_g[:, cs]).then_inc(S["b1_put"], 1)
            for half in range(2):
                x_low(0, 0, half)
            for e in range(E):
                dve.wait_ge(S["w_hi"], e + 1)
                low(w1_l[:, e, :], ps_h[:, e % RING, :], w1_h[:, e, :], S["w_lo"])
                if e == 0:
                    dve.wait_ge(S["wg_hi"], 1)
                    low(wg_l[:, :], ps_lg[:, 0:E], wg_h[:, :], S["wg_lo"])
            dve.wait_ge(S["wo_hi"], 1)
            low(wo_l[:, :, :], ps_y[:, 0:HC * D].rearrange("p (c d) -> p c d", c=HC), wo_h[:, :, :], S["wo_lo"])
            dve.wait_ge(S["const_ones"], 2 + E)
            for part_no in range(1, 12):
                route(part_no, 0, 0)
            dve.wait_ge(S["sq_hi"], 1)
            low(sq_l[:, :, :], sq_raw[:, :, :], sq_h[:, :, :], S["sq_lo"])
            dve.wait_ge(S["x_rest"], 16)
            ffn_steps(0, make_step(0), chain, dve.Fori)
            last_tiles(0)

            finished_statistics(TILES - 2)
            finished_statistics(TILES - 1)
            dve.wait_ge(S["x_stat"], TILES)
            for t in range(TILES):
                last = dve.bn_aggr(b_mean_var[:, t, :], b_stats[:, t, :])
            last.then_inc(S["a_stat"], 1)

            def side(u, b, bank=ps_t[:, :]):
                what, j = u
                if what == "xT":
                    dve.wait_ge(S["a_xh"], 2 * b + j + 1)
                    low(xT_l[:, j, :], bank, xT_h[:, j, :], S["a_xl"])
                elif what == "yT":
                    dve.wait_ge(S["yh_done"], CREDIT + 2 * b + j + 1)
                    wait_for(dve, S["yl_done"], CREDIT + 2 * b + j)
                    dve.tensor_scalar(yT[:, :], bank, gamma_col[:, :], beta_col[:, :], ALU.mult, ALU.add)\
                        .then_inc(S["yt_done"], 1)
                    dve.wait_ge(S["yt_done"], CREDIT + 2 * b + j + 1)
                    low(yT_l[:, :], yT[:, :], yT_h[:, :], S["yl_done"])
                elif what == "fc":
                    finish_x(b, j)
                else:
                    n = PROJECTIONS.index(u)
                    dve.wait_ge(S["pj_hi"], 6 * b + n + 1)
                    if what == "q":
                        hi, lo = (t[:, j * 512:(j + 1) * 512] for t in (q_h, q_l))
                    else:
                        pair = (k_h, k_l) if what == "k" else (v_h, v_l)
                        hi, lo = (part(t, slot(b, N) + j * 512, 512) for t in pair)
                    low(lo, bank, hi, S["pj_lo"])

            def maximum(b, i):
                dve.wait_ge(S["sc_done"], BT * b + i + 1)
                keys = (i + 1) * P
                s = ps_h[:, 2 * (i % 2):2 * (i % 2) + 2, :].rearrange("p a c -> p (a c)")[:, 0:keys]
                chain.step(dve.tensor_reduce(row_max[:, i:i + 1], s, AX.X, ALU.max))
                chain.wait()
                dve.tensor_scalar(neg_max[:, i:i + 1], row_max[:, i:i + 1], -SCALE, None, ALU.mult)\
                    .then_inc(S["max_done"], 1)

            def pT_low(b, i):
                for c in range(i // 4 + 1):
                    g = pT_count(i) + c
                    w = min(4, i + 1 - 4 * c) * P
                    dve.wait_ge(S["ph_done"], 12 * b + g + 1)
                    low(pT_l[:, g % 4, 0:w], ps_p[g % 2][:, 0:w], pT_h[:, g % 4, 0:w], S["pl_done"])

            def rows(b, i):
                dve.wait_ge(S["exp_done"], CREDIT + BT * b + i + 1)
                chain.step(dve.reciprocal(row_inv[:, i:i + 1], row_sum[:, i:i + 1]))
                chain.wait()
                dve.wait_ge(S["pv_done"], CREDIT + BT * b + i + 1)
                dve.wait_ge(S["vf_done"], CREDIT + 2 * b + i // MT + 1)
                dve.scalar_tensor_tensor(out=y[:, i, :], in0=ps_y[:, 0:D], scalar=row_inv[:, i:i + 1],
                                         in1=part(v_f, slot(b, N) + i * D, D), op0=ALU.mult, op1=ALU.add)\
                    .then_inc(S["yrow_done"], 1)
                dve.wait_ge(S["yrow_done"], CREDIT + BT * b + i + 1)
                chain.step(dve.bn_stats(y_stats[:, i % MT, :], y[:, i, :]))
                if i % MT == MT - 1:
                    chain.wait()
                    dve.tensor_copy(wait_carrier[:, :], y_stats[:, 0, 0:1])
                    for t in range(MT):
                        last = dve.bn_aggr(y_mean_var[:, t, :], y_stats[:, t, :])
                    last.then_inc(S["y_stat"], 1)

            def y_norm(b, j):
                dve.wait_ge(S["y_rs"], 2 * b + j + 1)
                wait_for(dve, S["yT_done"], CREDIT + 2 * b + j)
                for t in range(MT):
                    last = dve.tensor_scalar(yn[:, t, :], y[:, j * MT + t, :], y_mean_var[:, t, 0:1],
                                             y_rstd[:, t:t + 1], ALU.subtract, ALU.mult)
                last.then_inc(S["yn_done"], 1)

            def finish_x(b, j):
                dve.wait_ge(S["fc_done"], CREDIT + 2 * b + j + 1)
                dve.wait_ge(S["xb_done"], 2 * b + j + 1)
                dve.tensor_tensor(x[:, bass.ds(b * BT + j * MT, MT), :],
                                  ps_t[:, :].rearrange("p (t d) -> p t d", t=MT), x_bfc[:, :, :], ALU.add)\
                    .then_inc(S["xa_done"], 1)

            def step_a(n, b, more):
                def side_at(place):
                    unit = side_unit(n, b, more, place)
                    if unit:
                        side(*unit)
                side_at(0)
                pT_low(*at(n, b))
                if n + 2 < BT or more:
                    maximum(*at(n + 2, b))
                side_at(1)
                if (n != BT or begun(b)):
                    rows(*at(n - 1, b))
                if n == 5 or n == 9 and begun(b):
                    y_norm(b, (n - 5) // 4)
                side_at(2)

            for n, u in enumerate(FIRST_UNITS):
                side(u, 0, first_banks[n])
            maximum(0, 0)
            maximum(0, 1)
            attention_steps(step_a, chain, dve.Fori)
            rows(B - 1, BT - 1)
            y_norm(B - 1, 1)
            side(("yT", 1), B - 1)
            side(("fc", 1), B - 1)

            dve.wait_ge(S["xa_done"], CREDIT + 2 * B)
            for t in range(MT + 1):
                statistics(0, t)
            for t in range(MT):
                normalise(MACROS, 0, t)
            for half in range(2):
                x_low(MACROS, 0, half)
            for part_no in range(1, 12):
                route(part_no, MACROS, 0)
            ffn_steps(1, make_step(1), chain, dve.Fori)
            last_tiles(1)


_INS = ["L0_attn_x", "L0_attn_Wq", "L0_attn_Wk", "L0_attn_Wv", "L0_attn_Wfc", "L0_attn_bfc", "L0_attn_gamma",
        "L0_attn_beta", "L0_ffn_Wg", "L0_ffn_W1", "L0_ffn_b1", "L0_ffn_Wo", "L0_ffn_bo"]


def kernel(**inputs):
    import numpy as _np
    import concourse.bacc as _bacc
    from concourse import mybir as _mybir
    from concourse.bass_utils import run_bass_kernel_spmd as _run

    nc = _bacc.Bacc("TRN2", target_bir_lowering=False, num_devices=1)
    arrays, args = {}, []
    for name in _INS:
        a = _np.ascontiguousarray(inputs[name])
        arrays[f"in_{name}_dram"] = a
        args.append(nc.dram_tensor(f"in_{name}_dram", a.shape, _mybir.dt.from_np(a.dtype), kind="ExternalInput").ap())
    shape = inputs["L0_attn_x"].shape
    args.append(nc.dram_tensor("out_0_dram", shape, _mybir.dt.float32, kind="ExternalOutput").ap())
    macaron_kernel(nc, *args)
    r = _run(nc, [arrays], core_ids=[0])
    return r.results[0]["out_0_dram"]
```

```python
from contextlib import ExitStack

import concourse.bass as bass
from concourse import mybir

F32 = mybir.dt.float32
F32R = mybir.dt.float32r
U32 = mybir.dt.uint32
ALU = mybir.AluOpType
ACT = mybir.ActivationFunctionType
AX = mybir.AxisListType

P = 128
LN_EPS = 1e-05
TOPK_EPS = 1e-09
MASKED = -1e30
RING = 4
CREDIT = 1


class Chain:

    def __init__(self, eng, sem):
        self.eng, self.sem, self.base, self.n = eng, sem, 0, 0

    def step(self, ins):
        ins.then_inc(self.sem, 1)
        self.n += 1

    def wait(self):
        self.eng.wait_ge(self.sem, self.base + self.n)


def wait_for(eng, sem, count):
    if not (isinstance(count, int) and count <= 0):
        eng.wait_ge(sem, count)


def pT_count(n):
    return sum(t // 4 + 1 for t in range(max(n, 0)))


def pv_before(g):
    n = 0
    while pT_count(n + 1) <= g:
        n += 1
    return n + 1


SIDE = {(4, 0): ("xT", 0), (4, 2): ("q", 0), (5, 1): ("k", 0), (6, 1): ("v", 0), (7, 1): ("yT", 0),
        (8, 0): ("xT", 1), (8, 1): ("fc", 0), (8, 2): ("q", 1), (9, 1): ("k", 1), (9, 2): ("v", 1),
        (10, 1): ("yT", 1), (11, 1): ("fc", 1)}
IN_PS_G = [("xT", 1), ("k", 1), ("yT", 1)]
PROJECTIONS = [("q", 0), ("k", 0), ("v", 0), ("q", 1), ("k", 1), ("v", 1)]
OWN = ("yT", "fc")
AHEAD = 4


def macaron_kernel(nc, x_in, wq, wk, wv, wfc, bfc, gamma, beta, wg, w1, b1, wo, bo, out):
    B, N, D = x_in.shape
    E, H2, _ = w1.shape
    H = H2 // 2
    HC = H // P
    TILES = B * N // P
    MT = 4
    MACROS = TILES // MT
    BT = N // P
    SCALE = 1.0 / float(D) ** 0.5
    assert D == P and H2 == 512 and E == 8 and BT == 2 * MT

    x_tiles = x_in.rearrange("b (t p) d -> p (b t) d", p=P)
    out_tiles = out.rearrange("b (t p) d -> p (b t) d", p=P)

    with ExitStack() as ctx:
        def sb(name, shape, dt=F32):
            return ctx.enter_context(nc.sbuf_tensor(name, shape, dt))

        def ps(name, shape):
            return ctx.enter_context(nc.psum_tensor(name, shape, F32))

        def sem(name):
            return ctx.enter_context(nc.semaphore(name))

        x = sb("x", [P, TILES, D])
        ident = sb("ident", [P, P])
        ident_r = sb("ident_r", [P, P], F32R)
        causal_f = sb("causal_f", [P, P])
        causal_r = sb("causal_r", [P, P], F32R)
        expert_no = sb("expert_no", [P, MT, E])
        minus_half = sb("minus_half", [P, TILES])
        ln_eps = sb("ln_eps", [P, TILES])
        minus_one = sb("minus_one", [P, MT])
        bo_rows = sb("bo_rows", [P, D])
        bfc_rows = sb("bfc_rows", [P, D])
        gamma_col = sb("gamma_col", [P, 1])
        beta_col = sb("beta_col", [P, 1])
        last_col = sb("last_col", [P, E * MT])
        w1_rows = sb("w1_rows", [P, E * MT, D])
        b1_rows = sb("b1_rows", [E * MT, P])
        wg_rows = sb("wg_rows", [E, D])
        wo_rows = sb("wo_rows", [D, H])
        sq_raw = sb("sq_raw", [P, 4, D])
        w1_h = sb("w1_h", [P, E, H2], F32R)
        w1_l = sb("w1_l", [P, E, H2], F32R)
        wg_hl = sb("wg_hl", [P, 2 * E], F32R)
        wo_hl = sb("wo_hl", [P, HC, 2 * D], F32R)
        wg_h, wg_l = wg_hl[:, 0:E], wg_hl[:, E:2 * E]
        wo_h, wo_l = wo_hl[:, :, 0:D], wo_hl[:, :, D:2 * D]
        wfc_gamma = sb("wfc_gamma", [P, D])
        beta_rows = sb("beta_rows", [P, P])
        sq_h = sb("sq_h", [P, 4, D], F32R)
        sq_l = sb("sq_l", [P, 4, D], F32R)
        stats = sb("stats", [P, MT, 6])
        wait_carrier = sb("wait_carrier", [P, 1])
        mean_var = sb("mean_var", [P, MT, 2])
        var_eps = sb("var_eps", [P, MT])
        rstd = sb("rstd", [P, MT])
        neg_mean = sb("neg_mean", [P, MT])
        shift = sb("shift", [P, MT])
        xn = sb("xn", [P, MT, D])
        xn_half = sb("xn_half", [P, 2, MT, D])
        b_stats = sb("b_stats", [P, TILES, 6])
        b_mean_var = sb("b_mean_var", [P, TILES, 2])
        b_var_eps = sb("b_var_eps", [P, TILES])
        b_rstd = sb("b_rstd", [P, TILES])
        xT_h = sb("xT_h", [P, 2, MT * P], F32R)
        xT_l = sb("xT_l", [P, 2, MT * P], F32R)
        logits = sb("logits", [P, MT, E])
        top8 = sb("top8", [P, MT, 8])
        top_at = sb("top_at", [P, MT, 8], U32)
        below_max = sb("below_max", [P, MT, E])
        sig_pos = sb("sig_pos", [P, MT, E])
        sig_neg = sb("sig_neg", [P, MT, E])
        expo = sb("expo", [P, MT, E])
        is_first = sb("is_first", [P, MT, E])
        is_second = sb("is_second", [P, MT, E])
        chosen = sb("chosen", [P, MT, E])
        exp_all = sb("exp_all", [P, MT, E])
        exp_top = sb("exp_top", [P, MT, E])
        z_inv = sb("z_inv", [P, MT])
        z_all = sb("z_all", [P, MT])
        z_top = sb("z_top", [P, MT])
        z_den = sb("z_den", [P, MT])
        comb = sb("comb", [P, 2, MT, E])
        comb_sum = sb("comb_sum", [P, 2, MT])
        gate = sb("gate", [P, RING, H])
        gated = sb("gated", [P, 2, E, H])
        g_sum = sb("g_sum", [P, 2, H])
        gT_h = sb("gT_h", [P, HC * P], F32R)
        gT_l = sb("gT_l", [P, HC * P], F32R)
        bo_comb = sb("bo_comb", [P, MT, D])
        resid = sb("resid", [P, 2, MT, D])
        q_h = sb("q_h", [P, N], F32R)
        q_l = sb("q_l", [P, N], F32R)
        k_h = sb("k_h", [P, 2 * N], F32R)
        k_l = sb("k_l", [P, 2 * N], F32R)
        v_hl = sb("v_hl", [P, 2 * BT * 2 * D], F32R)
        v_f = sb("v_f", [P, 2 * BT * D])
        row_max = sb("row_max", [P, BT])
        neg_max = sb("neg_max", [P, BT])
        row_sum = sb("row_sum", [P, BT])
        row_inv = sb("row_inv", [P, BT])
        probs = w1_rows[:, 0:2 * BT, :].rearrange("p (a t) d -> p a (t d)", a=2)
        pT_h = sb("pT_h", [P, 4, MT * P], F32R)
        pT_l = sb("pT_l", [P, 4, MT * P], F32R)
        y = w1_rows[:, 2 * BT:3 * BT, :]
        y_stats = sb("y_stats", [P, MT, 6])
        y_mean_var = sb("y_mean_var", [P, MT, 2])
        y_var_eps = sb("y_var_eps", [P, MT])
        y_rstd = sb("y_rstd", [P, MT])
        y_neg_mean = sb("y_neg_mean", [P, MT])
        y_shift = sb("y_shift", [P, MT])
        yn = sb("yn", [P, MT, D])
        yT_h = sb("yT_h", [P, MT * P], F32R)
        yT_l = sb("yT_l", [P, MT * P], F32R)
        x_bfc = sb("x_bfc", [P, MT, D])

        ps_h = ps("ps_h", [P, RING, 512])
        ps_t = ps("ps_t", [P, 512])
        ps_lg = ps("ps_lg", [P, 512])
        ps_g = ps("ps_g", [P, 512])
        ps_y = ps("ps_y", [P, 512])
        ps_p = [ps_lg, ps_g]
        first_bank = {("xT", 0): ps_t[:, :], ("xT", 1): ps_t[:, :], ("q", 0): ps_t[:, :], ("k", 0): ps_lg[:, :],
                      ("v", 0): ps_lg[:, :], ("q", 1): ps_h[:, 1, :], ("k", 1): ps_h[:, 3, :], ("v", 1): ps_t[:, :]}

        names = """x_first x_rest w1_in0 w1_in1 w1_in2 w1_in3 b1_in small_in sq_in rows_in const_id
            const_ones wprep last_col w1_sub_pool w1_sub_dve w_tp w_hi w_lo wg_tp wg_hi wg_lo wo_tp wo_hi
            wo_lo b1_t b1_put sq_hi sq_lo setup_dve stat_done rstd_done xn_done xT_done xh_done xl_done
            lg_done lgc_done below_done sig_done comb_done fc_prep bo_done resid_done h_done gate_done
            gated_done gsum_done gT_done gh_done gl_done y_done x_done x_stat a_stat a_rstd first_xn a_xn
            a_xT a_xh a_xl pj_done pj_hi pj_lo vf_done sc_done max_done exp_done pT_done ph_done pl_done
            pv_done yrow_done y_stat y_rs yn_done yT_done yh_done yl_done fc_done xb_done xa_done out_done
            dve_chain pool_chain""".split()
        S = {n: sem(n) for n in names}
        block = ctx.enter_context(nc.Block())

        @block.sync
        def _(sp):
            w1_blocks = w1.rearrange("e (j p) d -> p (e j) d", p=P)
            sp.dma_start(x[:, 0:MT, :], x_tiles[:, 0:MT, :]).then_inc(S["x_first"], 16)
            for c in range(4):
                cs = slice(c * 2 * MT, (c + 1) * 2 * MT)
                sp.dma_start(w1_rows[:, cs, :], w1_blocks[:, cs, :]).then_inc(S[f"w1_in{c}"], 16)
            for n, w in enumerate((wq, wk, wv, wfc)):
                sp.dma_start(sq_raw[:, n, :], w).then_inc(S["sq_in"], 16)
            for rows, vector in ((bfc_rows, bfc), (bo_rows, bo)):
                sp.dma_start(rows[:, :], vector.rearrange("(a d) -> a d", a=1).to_broadcast([P, D]))\
                    .then_inc(S["rows_in"], 16)
            for col, vector in ((gamma_col, gamma), (beta_col, beta)):
                sp.dma_start(col[:, :], vector.rearrange("(p a) -> p a", a=1)).then_inc(S["rows_in"], 16)
            sp.dma_start(x[:, MT:TILES, :], x_tiles[:, MT:TILES, :]).then_inc(S["x_rest"], 16)
            for m in range(MACROS):
                sp.wait_ge(S["x_done"], CREDIT + TILES + MT * (m + 1))
                sp.dma_start(out_tiles[:, m * MT:(m + 1) * MT, :], x[:, m * MT:(m + 1) * MT, :])\
                    .then_inc(S["out_done"], 16)
            sp.wait_ge(S["out_done"], 16 * MACROS)

        def pool_rstd(pool, chain, var, eps_out, result, done):
            n = var.shape[1]
            chain.step(pool.tensor_tensor(eps_out, var, ln_eps[:, 0:n], ALU.add))
            chain.wait()
            pool.tensor_tensor(result, eps_out, minus_half[:, 0:n], ALU.pow).then_inc(done, 1)

        def ffn_steps(phase, step, chain, loop):
            t0 = phase * TILES
            m0 = phase * MACROS
            passes = TILES // 8 - 1
            for k in range(2):
                step(k, t0 + k, m0, 1)
            start = chain.n if chain else 0
            with loop(0, passes) as i:
                if chain:
                    per = chain_per_loop[chain.sem.name]
                    chain.base, chain.n = start + i * per, 0
                for k in range(2, 10):
                    step(k, t0 + i * 8 + k, m0 + i * 2 + k // MT, i * 2 + (k // MT + 1))
                if chain:
                    assert chain.n == per, (chain.sem.name, chain.n)
            if chain:
                chain.base, chain.n = 0, start + passes * per
            for k in range(2, 8):
                m = passes * 2 + k // MT
                step(k, t0 + passes * 8 + k, m0 + m, m + 1 if k < MT else None)

        def attention_steps(step, chain, loop):
            for n in range(AHEAD):
                step(n + BT, -1, True)
            start = chain.n if chain else 0
            with loop(0, B - 1) as b:
                if chain:
                    per = chain_per_attention[chain.sem.name]
                    chain.base, chain.n = start + b * per, 0
                for n in range(AHEAD, AHEAD + BT):
                    step(n, b, True)
                if chain:
                    assert chain.n == per, (chain.sem.name, chain.n)
            if chain:
                chain.base, chain.n = 0, start + (B - 1) * per
            for n in range(AHEAD, BT):
                step(n, B - 1, False)

        chain_per_loop = {"dve_chain": 2 * 17 + 8, "pool_chain": 8 * 3 + 2 * 2}
        chain_per_attention = {"dve_chain": 4 * 8, "pool_chain": 2 + 2 * 2}

        def at(n, b):
            return (b + 1, n - BT) if n >= BT else (b, n)

        def before_attention(tg, nxt):
            return nxt is None and tg < TILES

        def after_attention(tg):
            return isinstance(tg, int) and tg in (TILES, TILES + 1)

        def begun(b):
            return not (isinstance(b, int) and b < 0)

        def slot(b, size):
            return (b % 2) * size

        def v_half(b, j, low):
            both = part(v_hl, slot(b, BT * 2 * D) + j * MT * 2 * D, MT * 2 * D)
            return both.rearrange("p (t h d) -> p t h d", t=MT, h=2)[:, :, low, :]

        def side_unit(n, b, more, place):
            u = SIDE.get((n, place))
            if u and begun(b) and (more or u[0] in OWN):
                return u, (b if u[0] in OWN else b + 1), (ps_g if more and u in IN_PS_G else ps_t)[:, :]
            return None

        def part(t, lo, n):
            return t[:, lo:lo + n] if isinstance(lo, int) else t[:, bass.ds(lo, n)]

        @block.gpsimd
        def _(pool):
            chain = Chain(pool, S["pool_chain"])
            for name in ("gsum_done", "vf_done", "resid_done", "y_rs"):
                pool.sem_inc(S[name], CREDIT)
            pool.dma_start(b1_rows[:, :], b1.rearrange("e (j p) -> (e j) p", p=P)).then_inc(S["b1_in"], 16)
            pool.memset(ident[:, :], 0.0).then_inc(S["const_id"], 1)
            pool.memset(causal_f[:, :], 0.0).then_inc(S["const_id"], 1)
            pool.memset(minus_half[:, :], -0.5).then_inc(S["const_ones"], 1)
            pool.memset(ln_eps[:, :], LN_EPS).then_inc(S["const_ones"], 1)
            pool.memset(minus_one[:, :], -1.0).then_inc(S["const_ones"], 1)
            pool.wait_ge(S["const_id"], 2)
            pool.affine_select(out=ident[:, :], in_=ident[:, :], compare_op=ALU.not_equal, fill=1.0, base=0,
                               pattern=[[-1, P]], channel_multiplier=1).then_inc(S["const_id"], 1)
            pool.affine_select(out=causal_f[:, :], in_=causal_f[:, :], compare_op=ALU.is_ge, fill=MASKED, base=0,
                               pattern=[[-1, P]], channel_multiplier=1).then_inc(S["const_id"], 1)
            for e in range(E):
                pool.memset(expert_no[:, :, e:e + 1], float(e)).then_inc(S["const_ones"], 1)
            pool.wait_ge(S["const_ones"], 3)

            def scale_and_shift(mv, eps_out, neg_out, scale, shift_out, done):
                pool.tensor_tensor(eps_out[:, :], mv[:, :, 1], ln_eps[:, 0:MT], ALU.add)
                chain.step(pool.tensor_tensor(neg_out[:, :], mv[:, :, 0], minus_one[:, :], ALU.mult))
                chain.wait()
                chain.step(pool.tensor_tensor(scale[:, :], eps_out[:, :], minus_half[:, 0:MT], ALU.pow))
                chain.wait()
                pool.tensor_tensor(shift_out[:, :], neg_out[:, :], scale[:, :], ALU.mult).then_inc(done, 1)

            def prep(mg):
                pool.wait_ge(S["stat_done"], mg + 1)
                wait_for(pool, S["xn_done"], mg)
                scale_and_shift(mean_var, var_eps, neg_mean, rstd, shift, S["rstd_done"])

            def residual(k, tg, tile):
                pool.wait_ge(S["bo_done"], tg + 1)
                wait_for(pool, S["x_done"], CREDIT + tg - 2)
                xt = x[:, tile:tile + 1, :] if isinstance(tile, int) else x[:, bass.ds(tile, 1), :]
                t = k % MT
                pool.tensor_tensor(resid[:, (k // MT) % 2, t:t + 1, :], xt, bo_comb[:, t:t + 1, :], ALU.add)\
                    .then_inc(S["resid_done"], 1)

            prep(0)
            for c in (0, 2):
                lo, hi = c * 2 * MT, (c + 1) * 2 * MT
                pool.wait_ge(S["last_col"], c + 1)
                pool.tensor_tensor(w1_rows[:, lo:hi, 0:D - 1], w1_rows[:, lo:hi, 0:D - 1],
                                   last_col[:, lo:hi, None].to_broadcast([P, hi - lo, D - 1]),
                                   ALU.subtract).then_inc(S["w1_sub_pool"], 1)

            def batches_rstd(lo, hi, count):
                pool.wait_ge(S["a_stat"], count)
                pool_rstd(pool, chain, b_mean_var[:, lo:hi, 1], b_var_eps[:, lo:hi], b_rstd[:, lo:hi], S["a_rstd"])

            def make_step(phase):
                def step(k, tg, mg, nxt):
                    residual(k, tg, tg - phase * TILES)
                    g = gated[:, k % 2]
                    for e in range(2, E, 2):
                        pool.wait_ge(S["gated_done"], E * tg + e + 2)
                        chain.step(pool.tensor_tensor(g[:, 0:2, :], g[:, 0:2, :], g[:, e:e + 2, :], ALU.add))
                        chain.wait()
                    wait_for(pool, S["gT_done"], CREDIT + tg - 1)
                    pool.tensor_tensor(g_sum[:, k % 2, :], g[:, 0, :], g[:, 1, :], ALU.add)\
                        .then_inc(S["gsum_done"], 1)
                    if k % MT == 0 and nxt is not None:
                        prep(mg + 1)
                    if k == MT and before_attention(tg, nxt):
                        batches_rstd(0, BT, 1)
                return step

            ffn_steps(0, make_step(0), chain, pool.Fori)

            def half_norm(b, j):
                pool.wait_ge(S["a_xT"], 2 * b + j - 1)
                tile = b * BT + j * MT
                mean, inv = (t[:, bass.ds(tile, MT)] for t in (b_mean_var[:, :, 0], b_rstd[:, :]))
                rows = x[:, bass.ds(tile, MT), :]
                chain.step(pool.tensor_tensor(xn_half[:, j, :, :], rows,
                                              mean[:, :, None].to_broadcast([P, MT, D]), ALU.subtract))
                chain.wait()
                pool.tensor_tensor(xn_half[:, j, :, :], xn_half[:, j, :, :],
                                   inv[:, :, None].to_broadcast([P, MT, D]), ALU.mult).then_inc(S["a_xn"], 1)

            def v_sum(b, j):
                pool.wait_ge(S["pj_lo"], CREDIT + 6 * b + 3 * j + 3)
                pool.wait_ge(S["xa_done"], CREDIT + (2 * b - 2 if not isinstance(b, int) else max(2 * b - 2, 0)))
                lo = slot(b, BT * D) + j * MT * D
                pool.tensor_tensor(part(v_f, lo, MT * D).rearrange("p (t d) -> p t d", t=MT),
                                   v_half(b, j, 0).bitcast(F32), v_half(b, j, 1).bitcast(F32), ALU.add)\
                    .then_inc(S["vf_done"], 1)

            def add_bfc(b, j):
                wait_for(pool, S["xa_done"], CREDIT + 2 * b + j)
                pool.tensor_tensor(x_bfc[:, :, :], x[:, bass.ds(b * BT + j * MT, MT), :],
                                   bfc_rows[:, None, :].to_broadcast([P, MT, D]), ALU.add)\
                    .then_inc(S["xb_done"], 1)

            def y_rstd_of(b, j):
                pool.wait_ge(S["y_stat"], 2 * b + j + 1)
                wait_for(pool, S["yn_done"], CREDIT + 2 * b + j)
                scale_and_shift(y_mean_var, y_var_eps, y_neg_mean, y_rstd, y_shift, S["y_rs"])

            def step_a(n, b, more):
                if n == 4 and more:
                    half_norm(b + 1, 0)
                    half_norm(b + 1, 1)
                if n == 4 and not more:
                    prep(MACROS)
                if n == 4:
                    y_rstd_of(b, 0)
                    add_bfc(b, 0)
                if n == 7 and more:
                    v_sum(b + 1, 0)
                if n == 8 and begun(b):
                    y_rstd_of(b, 1)
                    add_bfc(b, 1)
                if n == 10 and begun(b):
                    v_sum(b + 1, 1)

            v_sum(0, 0)
            v_sum(0, 1)
            batches_rstd(BT, TILES, 4)
            pool.wait_ge(S["a_rstd"], 2)
            pool.wait_ge(S["x_done"], CREDIT + TILES)
            attention_steps(step_a, chain, pool.Fori)
            y_rstd_of(B - 1, 1)
            add_bfc(B - 1, 1)
            ffn_steps(1, make_step(1), chain, pool.Fori)

        @block.scalar
        def _(act):
            for name in ("exp_done", "yh_done", "yn_done"):
                act.sem_inc(S[name], CREDIT)
            act.dma_start(wg_rows[:, :], wg).then_inc(S["small_in"], 16)
            act.dma_start(wo_rows[:, :], wo).then_inc(S["small_in"], 16)

            def xh(mg, parity):
                act.wait_ge(S["xT_done"], mg + 1)
                if not (isinstance(mg, int) and mg < 2):
                    act.wait_ge(S["h_done"], CREDIT + 4 * E * (mg - 1))
                act.activation(xT_h[:, parity, :], ps_t[:, :], ACT.Copy).then_inc(S["xh_done"], 1)

            def normalise(mg, tile0, t):
                if t == 0:
                    act.wait_ge(S["rstd_done"], mg + 1)
                    wait_for(act, S["xT_done"], mg)
                tile = tile0 + t
                row = x[:, tile, 0:D - 1] if isinstance(tile, int) else x[:, bass.ds(tile, 1), 0:D - 1]
                dst = xn[:, t, 0:D - 1] if isinstance(tile, int) else xn[:, t:t + 1, 0:D - 1]
                ins = act.activation(dst, row, ACT.Identity, bias=shift[:, t:t + 1], scale=rstd[:, t:t + 1])
                if t == MT - 1:
                    ins.then_inc(S["xn_done"], 1)

            def sigmoids(mg):
                act.wait_ge(S["below_done"], mg + 1)
                wait_for(act, S["comb_done"], mg)
                act.activation(sig_pos[:, :, :], below_max[:, :, :], ACT.Sigmoid)
                act.activation(sig_neg[:, :, :], below_max[:, :, :], ACT.Sigmoid, scale=-1.0)\
                    .then_inc(S["sig_done"], 1)

            def bo_part(k, tg, mg):
                if k % MT == 0:
                    act.wait_ge(S["comb_done"], mg + 1)
                wait_for(act, S["resid_done"], CREDIT + tg - 1)
                t = k % MT
                act.activation(bo_comb[:, t, :], bo_rows[:, :], ACT.Copy, scale=comb_sum[:, (k // MT) % 2, t:t + 1])\
                    .then_inc(S["bo_done"], 1)

            def gh(tg):
                act.wait_ge(S["gT_done"], CREDIT + tg + 1)
                wait_for(act, S["y_done"], CREDIT + tg)
                act.activation(gT_h[:, :], ps_g[:, 0:HC * P], ACT.Copy).then_inc(S["gh_done"], 1)

            def step(k, tg, mg, nxt):
                for e in range(E):
                    n = E * tg + e
                    act.wait_ge(S["h_done"], CREDIT + n + 1)
                    wait_for(act, S["gated_done"], n - RING + 1)
                    act.activation(gate[:, e % RING, :], ps_h[:, e % RING, H:2 * H], ACT.Sigmoid)\
                        .then_inc(S["gate_done"], 1)
                    if e == 1:
                        bo_part(k, tg, mg)
                    if e == 6 and k > 0:
                        gh(tg - 1)
                    if nxt is not None:
                        if k % MT == 1 and e > MT:
                            normalise(mg + 1, nxt * MT, e - MT - 1)
                            if e == E - 1:
                                normalise(mg + 1, nxt * MT, MT - 1)
                        if k % MT == 2 and e == 3:
                            xh(mg + 1, (k // MT + 1) % 2)
                        if k % MT == 3 and e == 3:
                            sigmoids(mg + 1)
                    elif before_attention(tg, nxt) and (k, e) in ((6, 4), (7, 2), (7, 4)):
                        first({(6, 4): ("xT", 0), (7, 2): ("q", 0), (7, 4): ("k", 0)}[k, e])
                    if after_attention(tg) and (k, e) == (0, 3):
                        y_norm(B - 1, 1)
                    if after_attention(tg) and (k, e) == (0, 7):
                        side(("yT", 1), B - 1)

            def side(u, b, bank=ps_t[:, :]):
                what, j = u
                if what == "xT":
                    act.wait_ge(S["a_xT"], 2 * b + j + 1)
                    wait_for(act, S["pj_done"], CREDIT + 6 * b)
                    act.activation(xT_h[:, j, :], bank, ACT.Copy).then_inc(S["a_xh"], 1)
                elif what == "yT":
                    act.wait_ge(S["yT_done"], CREDIT + 2 * b + j + 1)
                    wait_for(act, S["fc_done"], CREDIT + 2 * b + j)
                    act.activation(yT_h[:, :], bank, ACT.Copy).then_inc(S["yh_done"], 1)
                else:
                    u = PROJECTIONS.index((what, j))
                    act.wait_ge(S["pj_done"], CREDIT + 6 * b + u + 1)
                    if what == "q":
                        wait_for(act, S["sc_done"], BT * b - (4 if j == 0 else 0))
                        dst = q_h[:, j * 512:(j + 1) * 512]
                    else:
                        wait_for(act, S["pv_done"], CREDIT + BT * (b - 1))
                        if what == "v":
                            wait_for(act, S["vf_done"], CREDIT + 2 * (b - 1))
                        dst = part(k_h, slot(b, N) + j * 512, 512)
                        if what == "v":
                            dst, bank = v_half(b, j, 0), bank.rearrange("p (t d) -> p t d", t=MT)
                    act.activation(dst, bank, ACT.Copy).then_inc(S["pj_hi"], 1)

            def y_norm(b, j):
                act.wait_ge(S["y_rs"], CREDIT + 2 * b + j + 1)
                wait_for(act, S["yT_done"], CREDIT + 2 * b + j)
                for t in range(MT):
                    last = act.activation(yn[:, t, :], y[:, j * MT + t, :], ACT.Identity,
                                          bias=y_shift[:, t:t + 1], scale=y_rstd[:, t:t + 1])
                last.then_inc(S["yn_done"], 1)

            def exp_tile(b, i):
                act.wait_ge(S["max_done"], BT * b + i + 1)
                wait_for(act, S["pT_done"], CREDIT + 12 * b + (pT_count(i - 1) if i >= 2 else pT_count(i + 7) - 12))
                wait_for(act, S["yrow_done"], CREDIT + BT * b + (i - BT + 1 if i < AHEAD else 0))
                keys = (i + 1) * P
                s = ps_h[:, 2 * (i % 2):2 * (i % 2) + 2, :].rearrange("p a c -> p (a c)")[:, 0:keys]
                act.activation(probs[:, i % 2, 0:keys], s, ACT.Exp, bias=neg_max[:, i:i + 1], scale=SCALE,
                               accum_out=row_sum[:, i:i + 1]).then_inc(S["exp_done"], 1)

            def pT_high(b, i):
                for c in range(i // 4 + 1):
                    g = pT_count(i) + c
                    w = min(4, i + 1 - 4 * c) * P
                    act.wait_ge(S["pT_done"], CREDIT + 12 * b + g + 1)
                    wait_for(act, S["pv_done"], CREDIT + BT * b + (pv_before(g - 4) if g >= 4 else
                                                                  pv_before(g + 8) - BT))
                    act.activation(pT_h[:, g % 4, 0:w], ps_p[c][:, 0:w], ACT.Copy).then_inc(S["ph_done"], 1)

            def step_a(n, b, more):
                few = n > BT
                if (n + 1 < BT or more) and not few:
                    exp_tile(*at(n + 1, b))
                early, middle, late = (side_unit(n, b, more, place) for place in range(3))
                if early:
                    side(*early)
                pT_high(*at(n, b))
                if few:
                    exp_tile(*at(n + 1, b))
                if middle and middle[0][0] != "fc":
                    side(*middle)
                if n == 6 or n == 9 and begun(b):
                    y_norm(b, int(n == 9))
                if n == 5 and not more:
                    for t in range(MT):
                        normalise(MACROS, 0, t)
                if n == 7 and not more:
                    xh(MACROS, 0)
                if late and late[0][0] != "fc":
                    side(*late)

            def first(u):
                if u[0] == "xT":
                    act.wait_ge(S["h_done"], CREDIT + MT * E * (MACROS - 1 + u[1]))
                side(u, 0, first_bank[u])

            act.wait_ge(S["const_id"], 4)
            act.activation(gate[:, 0, 0:P], ident[:, :], ACT.Sigmoid)
            act.wait_ge(S["setup_dve"], 1)
            for t in range(MT):
                normalise(0, 0, t)
            xh(0, 0)
            for e in range(E):
                act.wait_ge(S["w_tp"], e + 1)
                act.activation(w1_h[:, e, :], ps_h[:, e % RING, :], ACT.Copy).then_inc(S["w_hi"], 1)
                if e == 0:
                    act.wait_ge(S["wg_tp"], 1)
                    act.activation(wg_h, ps_lg[:, 0:E], ACT.Copy).then_inc(S["wg_hi"], 1)
                if e == 3:
                    act.wait_ge(S["sq_in"], 64)
                    act.wait_ge(S["rows_in"], 64)
                    act.activation(wfc_gamma[:, :], sq_raw[:, 3, :], ACT.Copy, scale=gamma_col[:, :])
                    act.activation(beta_rows[:, :], ident[:, :], ACT.Identity, bias=beta_col[:, :], scale=0.0)\
                        .then_inc(S["fc_prep"], 1)
                if e == 5:
                    sigmoids(0)
            act.wait_ge(S["wo_tp"], 1)
            act.activation(wo_h, ps_y[:, 0:HC * D].rearrange("p (c d) -> p c d", c=HC), ACT.Copy)\
                .then_inc(S["wo_hi"], 1)
            act.wait_ge(S["fc_prep"], 1)
            act.activation(sq_h[:, 0:3, :], sq_raw[:, 0:3, :], ACT.Copy)
            act.activation(sq_h[:, 3, :], wfc_gamma[:, :], ACT.Copy).then_inc(S["sq_hi"], 1)
            act.wait_ge(S["const_id"], 4)
            act.activation(ident_r[:, :], ident[:, :], ACT.Copy).then_inc(S["sq_hi"], 1)
            act.activation(causal_r[:, :], causal_f[:, :], ACT.Copy).then_inc(S["sq_hi"], 1)
            ffn_steps(0, step, None, act.Fori)
            for u in (("xT", 1), ("v", 0), ("q", 1), ("k", 1)):
                first(u)
            gh(TILES - 1)
            first(("v", 1))

            exp_tile(0, 0)
            attention_steps(step_a, None, act.Fori)
            sigmoids(MACROS)

            ffn_steps(1, step, None, act.Fori)
            gh(2 * TILES - 1)

        @block.tensor
        def _(pe):
            for name in ("gT_done", "h_done", "y_done", "pj_done", "pv_done", "pT_done", "fc_done", "yT_done"):
                pe.sem_inc(S[name], CREDIT)

            def product(dst, a_h, a_l, b_h, b_l, masked=None):
                pe.matmul(dst, a_h, b_h, start=True, stop=False)
                if masked is not None:
                    pe.matmul(masked, ident_r[:, :], causal_r[:, :], start=False, stop=False)
                pe.matmul(dst, a_h, b_l, start=False, stop=False)
                return pe.matmul(dst, a_l, b_h, start=False, stop=True)

            def transpose_rows(rows, done):
                for t in range(MT):
                    last = pe.transpose(ps_t[:, t * P:(t + 1) * P], rows(t), ident[:, :])
                last.then_inc(done, 1)

            def xT(mg):
                pe.wait_ge(S["xn_done"], mg + 1)
                wait_for(pe, S["xl_done"], mg)
                transpose_rows(lambda t: xn[:, t, :], S["xT_done"])

            def router(mg, parity):
                pe.wait_ge(S["xl_done"], mg + 1)
                wait_for(pe, S["lgc_done"], mg)
                for t in range(MT):
                    x_h, x_l = (rows[:, parity, t * P:(t + 1) * P] for rows in (xT_h, xT_l))
                    lo = 2 * E * t
                    pe.matmul(ps_lg[:, lo:lo + 2 * E], x_h, wg_hl[:, :], start=True, stop=False)
                    last = pe.matmul(ps_lg[:, lo:lo + E], x_l, wg_h, start=False, stop=True)
                last.then_inc(S["lg_done"], 1)

            def gT(k, tg):
                pe.wait_ge(S["gsum_done"], CREDIT + tg + 1)
                wait_for(pe, S["gl_done"], CREDIT + tg)
                for c in range(HC):
                    last = pe.transpose(ps_g[:, c * P:(c + 1) * P], g_sum[:, k % 2, c * P:(c + 1) * P], ident[:, :])
                last.then_inc(S["gT_done"], 1)

            def down(tg):
                pe.wait_ge(S["gl_done"], CREDIT + tg + 1)
                wait_for(pe, S["x_done"], CREDIT + tg)
                pe.matmul(ps_y[:, 0:2 * D], gT_h[:, 0:P], wo_hl[:, 0, :], start=True, stop=False)
                for c in range(HC):
                    pe.matmul(ps_y[:, 0:D], gT_l[:, c * P:(c + 1) * P], wo_h[:, c, :], start=False, stop=False)
                for c in range(1, HC):
                    last = pe.matmul(ps_y[:, 0:2 * D], gT_h[:, c * P:(c + 1) * P], wo_hl[:, c, :],
                                     start=False, stop=c == HC - 1)
                last.then_inc(S["y_done"], 1)

            def step(k, tg, mg, nxt):
                for e in range(E):
                    n = E * tg + e
                    wait_for(pe, S["gated_done"], n - RING + 1)
                    if k == 0 and isinstance(tg, int) and tg == 0:
                        pe.wait_ge(S["w_lo"], min(e + RING + 1, E))
                    ts = slice((k % MT) * P, (k % MT + 1) * P)
                    product(ps_h[:, e % RING, :], xT_h[:, (k // MT) % 2, ts], xT_l[:, (k // MT) % 2, ts],
                            w1_h[:, e, :], w1_l[:, e, :]).then_inc(S["h_done"], 1)
                    if e == 2 and k > 1:
                        down(tg - 2)
                    if nxt is not None:
                        if k % MT == 2 and e == 2:
                            xT(mg + 1)
                        if k % MT == 3 and e == 0:
                            router(mg + 1, (k // MT + 1) % 2)
                    if e == 6 and k > 0:
                        gT(k - 1, tg - 1)
                    if before_attention(tg, nxt) and (k, e) in ((6, 2), (7, 1), (7, 3), (7, 6)):
                        first({(6, 2): ("xT", 0), (7, 1): ("q", 0), (7, 3): ("k", 0), (7, 6): ("xT", 1)}[k, e])
                    if after_attention(tg) and (k, e) == (0, 7):
                        bank_free(("yT", 1), B - 1, False)
                        side(("yT", 1), B - 1)
                    if after_attention(tg) and (k, e) == (1, 4):
                        bank_free(("fc", 1), B - 1, False)
                        side(("fc", 1), B - 1)
                if after_attention(tg) and k == 1:
                    read_out(("fc", 1), B - 1)

            def read_out(u, b):
                what, j = u
                if what == "xT":
                    wait_for(pe, S["a_xl"], 2 * b + j + 1)
                elif what == "yT":
                    pe.wait_ge(S["yl_done"], CREDIT + 2 * b + j + 1)
                elif what == "fc":
                    pe.wait_ge(S["xa_done"], CREDIT + 2 * b + j + 1)
                else:
                    pe.wait_ge(S["pj_lo"], CREDIT + 6 * b + PROJECTIONS.index(u) + 1)

            def bank_free(u, b, more):
                order = [v for v in SIDE.values() if v in IN_PS_G] if more and u in IN_PS_G else \
                    [v for v in SIDE.values() if v not in IN_PS_G] if more else \
                    [("yT", 0), ("fc", 0), ("yT", 1), ("fc", 1)]
                if u == IN_PS_G[0] and more:
                    pe.wait_ge(S["pl_done"], 12 * b + 12)
                elif u == ("fc", 0) and not more:
                    pe.wait_ge(S["xl_done"], MACROS + 1)
                elif u == order[0]:
                    read_out(PROJECTIONS[-1], b)
                    wait_for(pe, S["xa_done"], CREDIT + 2 * b)
                else:
                    before = order[order.index(u) - 1]
                    read_out(before, b if before[0] in OWN else b + 1)

            def side(u, b, bank=ps_t[:, :]):
                what, j = u
                if what in ("xT", "yT"):
                    if what == "xT":
                        if isinstance(b, int):
                            pe.wait_ge(S["first_xn"], j + 1)
                        else:
                            pe.wait_ge(S["a_xn"], 2 * b + j - 1)
                        source = xn_half[:, j]
                    else:
                        pe.wait_ge(S["yn_done"], CREDIT + 2 * b + j + 1)
                        source = yn
                    for t in range(MT):
                        last = pe.transpose(bank[:, t * P:(t + 1) * P], source[:, t, :], ident[:, :])
                    last.then_inc(S["a_xT" if what == "xT" else "yT_done"], 1)
                    return
                if what == "fc":
                    pe.wait_ge(S["yl_done"], CREDIT + 2 * b + j + 1)
                    rows_h, rows_l, n, done = yT_h, yT_l, 3, S["fc_done"]
                else:
                    pe.wait_ge(S["a_xl"], 2 * b + j + 1)
                    rows_h, rows_l, n, done = xT_h[:, j, :], xT_l[:, j, :], "qkv".find(what), S["pj_done"]
                if what in ("v", "fc"):
                    for t in range(MT):
                        ts = slice(t * P, (t + 1) * P)
                        last = product(bank[:, ts], rows_h[:, ts], rows_l[:, ts], sq_h[:, n, :], sq_l[:, n, :])
                else:
                    last = product(bank[:, :], sq_h[:, n, :], sq_l[:, n, :], rows_h, rows_l)
                last.then_inc(done, 1)

            def scores(b, i):
                pe.wait_ge(S["pj_lo"], CREDIT + 6 * b + (2 if i < MT else 5))
                wait_for(pe, S["exp_done"], CREDIT + BT * b + i - 1)
                ns = slice(i * P, (i + 1) * P)
                for c in range(i // 4 + 1):
                    w = min(4, i + 1 - 4 * c) * P
                    lo = slot(b, N) + c * 512
                    bank = ps_h[:, 2 * (i % 2) + c, :]
                    last = product(bank[:, 0:w], q_h[:, ns], q_l[:, ns], part(k_h, lo, w), part(k_l, lo, w),
                                   bank[:, w - P:w] if c == i // 4 else None)
                last.then_inc(S["sc_done"], 1)

            def probs_T(b, i):
                pe.wait_ge(S["exp_done"], CREDIT + BT * b + i + 1)
                for c in range(i // 4 + 1):
                    g = pT_count(i) + c
                    if (i, c) == (4, 1):
                        pe.wait_ge(S["yl_done"], CREDIT + 2 * b)
                    else:
                        wait_for(pe, S["pl_done"], 12 * b + (pT_count(i - 1) + c + 1 if i else -1))
                    for kb in range(4 * c, min(4 * c + 4, i + 1)):
                        o = (kb - 4 * c) * P
                        last = pe.transpose(ps_p[c][:, o:o + P], probs[:, i % 2, kb * P:(kb + 1) * P], ident[:, :])
                    last.then_inc(S["pT_done"], 1)

            def pv(b, i):
                wait_for(pe, S["yrow_done"], CREDIT + BT * b + i)
                pe.wait_ge(S["pj_lo"], CREDIT + 6 * b + (3 if i < MT else 6))
                for kb in range(i + 1):
                    g = pT_count(i) + kb // 4
                    if kb % 4 == 0:
                        pe.wait_ge(S["pl_done"], 12 * b + g + 1)
                    o = (kb % 4) * P
                    a_h, a_l = pT_h[:, g % 4, o:o + P], pT_l[:, g % 4, o:o + P]
                    lo = slot(b, BT * 2 * D) + kb * 2 * D
                    pe.matmul(ps_y[:, 0:2 * D], a_h, part(v_hl, lo, 2 * D), start=kb == 0, stop=False)
                    last = pe.matmul(ps_y[:, 0:D], a_l, part(v_hl, lo, D), start=False, stop=kb == i)
                last.then_inc(S["pv_done"], 1)

            def step_a(n, b, more):
                def side_at(place):
                    unit = side_unit(n, b, more, place)
                    if unit:
                        bank_free(unit[0], b, more)
                        side(*unit)
                side_at(0)
                probs_T(*at(n, b))
                if n + 2 < BT or more:
                    scores(*at(n + 2, b))
                side_at(1)
                if (n != BT or begun(b)):
                    pv(*at(n - 1, b))
                if n == 7 and not more:
                    read_out(("yT", 0), b)
                    xT(MACROS)
                side_at(2)

            def first(u):
                if u == ("xT", 0):
                    pe.wait_ge(S["xl_done"], MACROS)
                elif u == ("xT", 1):
                    read_out(("q", 0), 0)
                elif u == ("q", 0):
                    pe.wait_ge(S["sq_hi"], 3)
                    pe.wait_ge(S["sq_lo"], 2)
                elif u == ("k", 0):
                    pe.wait_ge(S["lgc_done"], MACROS)
                elif u == ("v", 0):
                    read_out(("k", 0), 0)
                elif u[0] in "qk":
                    pe.wait_ge(S["gated_done"], E * TILES)
                side(u, 0, first_bank[u])

            pe.wait_ge(S["const_id"], 4)
            pe.wait_ge(S["b1_in"], 16)
            pe.transpose(ps_g[:, 0:E * MT], b1_rows[:, :], ident[0:E * MT, 0:E * MT]).then_inc(S["b1_t"], 1)
            xT(0)
            pe.wait_ge(S["wprep"], 2)
            pe.transpose(ps_lg[:, 0:E], wg_rows[:, :], ident[0:E, 0:E]).then_inc(S["wg_tp"], 1)
            for e in range(E):
                pe.wait_ge(S["w1_sub_dve" if e // 2 % 2 else "w1_sub_pool"], e // 4 + 1)
                pe.wait_ge(S["b1_put"], e // 2 + 1)
                if e >= RING:
                    pe.wait_ge(S["w_lo"], e - RING + 1)
                for j in range(MT):
                    last = pe.transpose(ps_h[:, e % RING, j * P:(j + 1) * P], w1_rows[:, e * MT + j, :], ident[:, :])
                last.then_inc(S["w_tp"], 1)
                if e == RING - 1:
                    pe.wait_ge(S["wg_lo"], 1)
                    router(0, 0)
            pe.wait_ge(S["small_in"], 32)
            for c in range(HC):
                pe.transpose(ps_y[:, c * D:(c + 1) * D], wo_rows[:, c * P:(c + 1) * P], ident[:, :])
            pe.wait_ge(S["fc_prep"], 1)
            last = pe.matmul(ps_y[:, HC * D:(HC + 1) * D], beta_rows[:, :], sq_raw[:, 3, :], start=True, stop=True)
            last.then_inc(S["wo_tp"], 1)
            ffn_steps(0, step, None, pe.Fori)
            first(("v", 0))
            down(TILES - 2)
            first(("q", 1))
            first(("k", 1))
            gT(7, TILES - 1)
            first(("v", 1))

            scores(0, 0)
            down(TILES - 1)
            scores(0, 1)
            read_out(PROJECTIONS[-1], 0)
            pe.wait_ge(S["x_done"], CREDIT + TILES)
            attention_steps(step_a, None, pe.Fori)
            pv(B - 1, BT - 1)
            router(MACROS, 0)
            bank_free(("fc", 0), B - 1, False)
            side(("fc", 0), B - 1)

            ffn_steps(1, step, None, pe.Fori)
            down(2 * TILES - 2)
            gT(7, 2 * TILES - 1)
            down(2 * TILES - 1)

        @block.vector
        def _(dve):
            chain = Chain(dve, S["dve_chain"])
            for name in ("gl_done", "x_done", "yrow_done", "xa_done", "pj_lo", "yl_done"):
                dve.sem_inc(S[name], CREDIT)

            def low(dst, src, high, done):
                dve.tensor_tensor(dst, src, high.bitcast(F32), ALU.subtract).then_inc(done, 1)

            def tile_of_x(t, cols=D):
                return x[:, t:t + 1, 0:cols] if isinstance(t, int) else x[:, bass.ds(t, 1), 0:cols]

            def statistics(mg, tile0, t):
                if t < MT:
                    chain.step(dve.bn_stats(stats[:, t, :], tile_of_x(tile0 + t)))
                    return
                chain.wait()
                wait_for(dve, S["rstd_done"], mg)
                dve.tensor_copy(wait_carrier[:, :], stats[:, 0, 0:1])
                for t in range(MT):
                    last = dve.bn_aggr(mean_var[:, t, :], stats[:, t, :])
                last.then_inc(S["stat_done"], 1)

            def x_low(mg, parity, half):
                if half == 0:
                    dve.wait_ge(S["xh_done"], mg + 1)
                cs = slice(half * 2 * P, (half + 1) * 2 * P)
                ins = dve.tensor_tensor(xT_l[:, parity, cs], ps_t[:, cs], xT_h[:, parity, cs].bitcast(F32),
                                        ALU.subtract)
                if half == 1:
                    ins.then_inc(S["xl_done"], 1)

            def route(part_no, mg, parity):
                if part_no == 1:
                    dve.wait_ge(S["lg_done"], mg + 1)
                    both = ps_lg[:, 0:2 * MT * E].rearrange("p (t h e) -> p t h e", t=MT, h=2)
                    chain.step(dve.tensor_copy(logits[:, :, :], both[:, :, 0, :]))
                    chain.wait()
                    dve.tensor_tensor(logits[:, :, :], logits[:, :, :], both[:, :, 1, :], ALU.add)\
                        .then_inc(S["lgc_done"], 1)
                    dve.wait_ge(S["lgc_done"], mg + 1)
                    dve.tensor_copy(wait_carrier[:, :], logits[:, 0, 0:1])
                    for t in range(MT):
                        ins = dve.max(top8[:, t, :], logits[:, t, :])
                    chain.step(ins)
                elif part_no == 2:
                    wait_for(dve, S["sig_done"], mg)
                    chain.wait()
                    dve.tensor_tensor(below_max[:, :, :], logits[:, :, :], top8[:, :, 0:1].to_broadcast([P, MT, E]),
                                      ALU.subtract).then_inc(S["below_done"], 1)
                    for t in range(MT):
                        ins = dve.max_index(top_at[:, t, :], top8[:, t, :], logits[:, t, :])
                    chain.step(ins)
                elif part_no == 3:
                    chain.wait()
                    chain.step(dve.tensor_tensor(is_first[:, :, :], expert_no[:, :, :],
                                                 top_at[:, :, 0:1].to_broadcast([P, MT, E]), ALU.is_equal))
                    chain.step(dve.tensor_tensor(is_second[:, :, :], expert_no[:, :, :],
                                                 top_at[:, :, 1:2].to_broadcast([P, MT, E]), ALU.is_equal))
                elif part_no == 4:
                    chain.wait()
                    chain.step(dve.tensor_tensor(chosen[:, :, :], is_first[:, :, :], is_second[:, :, :], ALU.add))
                elif part_no == 5:
                    dve.wait_ge(S["sig_done"], mg + 1)
                    chain.step(dve.reciprocal(expo[:, :, :], sig_neg[:, :, :]))
                elif part_no == 6:
                    chain.wait()
                    chain.step(dve.tensor_tensor(exp_all[:, :, :], expo[:, :, :], sig_pos[:, :, :], ALU.mult))
                elif part_no == 7:
                    chain.wait()
                    chain.step(dve.tensor_reduce(z_all[:, :], exp_all[:, :, :], AX.X, ALU.add))
                    chain.step(dve.tensor_tensor(exp_top[:, :, :], exp_all[:, :, :], chosen[:, :, :], ALU.mult))
                elif part_no == 8:
                    chain.wait()
                    chain.step(dve.tensor_reduce(z_top[:, :], exp_top[:, :, :], AX.X, ALU.add))
                elif part_no == 9:
                    chain.wait()
                    chain.step(dve.scalar_tensor_tensor(out=z_den[:, :], in0=z_all[:, :], scalar=TOPK_EPS,
                                                        in1=z_top[:, :], op0=ALU.mult, op1=ALU.add))
                elif part_no == 10:
                    chain.wait()
                    chain.step(dve.reciprocal(z_inv[:, :], z_den[:, :]))
                elif part_no == 11:
                    chain.wait()
                    dve.scalar_tensor_tensor(out=comb[:, parity, :, :], in0=exp_top[:, :, :], scalar=0.5,
                                             in1=z_inv[:, :, None].to_broadcast([P, MT, E]),
                                             op0=ALU.mult, op1=ALU.mult)
                    dve.scalar_tensor_tensor(out=comb_sum[:, parity, :], in0=z_top[:, :], scalar=0.5,
                                             in1=z_inv[:, :], op0=ALU.mult, op1=ALU.mult)\
                        .then_inc(S["comb_done"], 1)

            def g_low(tg):
                dve.wait_ge(S["gh_done"], tg + 1)
                low(gT_l[:, :], ps_g[:, 0:HC * P], gT_h[:, :], S["gl_done"])

            def finish_low(k, tg):
                dve.wait_ge(S["y_done"], CREDIT + tg + 1)
                dve.wait_ge(S["resid_done"], CREDIT + tg + 1)
                rows = resid[:, (k // MT) % 2, k % MT, :]
                chain.step(dve.tensor_tensor(rows, ps_y[:, D:2 * D], rows, ALU.add))

            def finish(k, tile):
                chain.wait()
                dve.tensor_tensor(tile_of_x(tile), ps_y[:, None, 0:D],
                                  resid[:, (k // MT) % 2, k % MT:k % MT + 1, :], ALU.add).then_inc(S["x_done"], 1)

            def finished_statistics(tile):
                dve.wait_ge(S["x_done"], CREDIT + tile + 1)
                dst = b_stats[:, tile:tile + 1, :] if isinstance(tile, int) else b_stats[:, bass.ds(tile, 1), :]
                dve.bn_stats(dst, tile_of_x(tile)).then_inc(S["x_stat"], 1)

            def make_step(phase):
                def step(k, tg, mg, nxt):
                    if k % MT == 0:
                        dve.wait_ge(S["comb_done"], mg + 1)
                    wait_for(dve, S["gsum_done"], CREDIT + tg - 1)
                    for e in range(E):
                        dve.wait_ge(S["gate_done"], E * tg + e + 1)
                        dve.scalar_tensor_tensor(
                            out=gated[:, k % 2, e, :], in0=ps_h[:, e % RING, 0:H],
                            scalar=comb[:, (k // MT) % 2, k % MT, e:e + 1],
                            in1=gate[:, e % RING, :], op0=ALU.mult, op1=ALU.mult).then_inc(S["gated_done"], 1)
                        if nxt is not None:
                            parity = (k // MT + 1) % 2
                            if k % MT == 0 and e <= MT:
                                statistics(mg + 1, nxt * MT, e)
                            if k % MT == 2 and e in (4, 5):
                                x_low(mg + 1, parity, e - 4)
                            if k % MT == 3:
                                for part_no in ((), (1,), (2,), (3,), (4, 5), (6, 7), (8, 9), (10, 11))[e]:
                                    route(part_no, mg + 1, parity)
                        if e == 6 and k > 0:
                            g_low(tg - 1)
                        if e == 4 and k > 1:
                            finish_low(k - 2, tg - 2)
                        if e == 5 and k > 1:
                            finish(k - 2, tg - 2 - phase * TILES)
                        if e == 7 and k > 1 and phase == 0:
                            finished_statistics(tg - 2)
                        if phase == 0 and k == 0 and e == E - 1:
                            dve.wait_ge(S["sq_hi"], 1)
                            low(sq_l[:, 0:3, :], sq_raw[:, 0:3, :], sq_h[:, 0:3, :], S["sq_lo"])
                            low(sq_l[:, 3, :], wfc_gamma[:, :], sq_h[:, 3, :], S["sq_lo"])
                        if before_attention(tg, nxt):
                            if (k, e) in ((4, 0), (4, 3), (4, 6)):
                                mean_variance(8 * (e // 3), 8 * (e // 3) + 8)
                            if (k, e) in ((5, 5), (5, 7), (6, 1), (6, 3)):
                                first_norm({(5, 5): 0, (5, 7): 2, (6, 1): 4, (6, 3): 6}[k, e])
                            if (k, e) in ((6, 6), (7, 3), (7, 5)):
                                first({(6, 6): ("xT", 0), (7, 3): ("q", 0), (7, 5): ("k", 0)}[k, e])
                        if after_attention(tg) and (k, e) == (0, 7):
                            side(("yT", 1), B - 1)
                        if after_attention(tg) and (k, e) == (1, 6):
                            side(("fc", 1), B - 1)
                return step

            def mean_variance(lo, hi):
                dve.wait_ge(S["x_stat"], hi)
                for t in range(lo, hi):
                    last = dve.bn_aggr(b_mean_var[:, t, :], b_stats[:, t, :])
                last.then_inc(S["a_stat"], 1)

            def first_norm(t0):
                dve.wait_ge(S["a_rstd"], 1)
                for t in (t0, t0 + 1):
                    ins = dve.tensor_scalar(xn_half[:, t // MT, t % MT, :], x[:, t, :], b_mean_var[:, t, 0:1],
                                            b_rstd[:, t:t + 1], ALU.subtract, ALU.mult)
                if t0 % MT == 2:
                    ins.then_inc(S["first_xn"], 1)

            def first(u):
                side(u, 0, first_bank[u])

            def side(u, b, bank=ps_t[:, :]):
                what, j = u
                if what == "xT":
                    dve.wait_ge(S["a_xh"], 2 * b + j + 1)
                    low(xT_l[:, j, :], bank, xT_h[:, j, :], S["a_xl"])
                elif what == "yT":
                    dve.wait_ge(S["yh_done"], CREDIT + 2 * b + j + 1)
                    low(yT_l[:, :], bank, yT_h[:, :], S["yl_done"])
                elif what == "fc":
                    finish_x(b, j)
                else:
                    n = PROJECTIONS.index(u)
                    dve.wait_ge(S["pj_hi"], 6 * b + n + 1)
                    if what == "q":
                        hi, lo = (t[:, j * 512:(j + 1) * 512] for t in (q_h, q_l))
                    else:
                        hi, lo = (part(t, slot(b, N) + j * 512, 512) for t in (k_h, k_l))
                        if what == "v":
                            hi, lo = v_half(b, j, 0), v_half(b, j, 1)
                            bank = bank.rearrange("p (t d) -> p t d", t=MT)
                    low(lo, bank, hi, S["pj_lo"])

            def maximum(b, i):
                dve.wait_ge(S["sc_done"], BT * b + i + 1)
                keys = (i + 1) * P
                s = ps_h[:, 2 * (i % 2):2 * (i % 2) + 2, :].rearrange("p a c -> p (a c)")[:, 0:keys]
                chain.step(dve.tensor_reduce(row_max[:, i:i + 1], s, AX.X, ALU.max))
                chain.wait()
                dve.tensor_scalar(neg_max[:, i:i + 1], row_max[:, i:i + 1], -SCALE, None, ALU.mult)\
                    .then_inc(S["max_done"], 1)

            def pT_low(b, i):
                for c in range(i // 4 + 1):
                    g = pT_count(i) + c
                    w = min(4, i + 1 - 4 * c) * P
                    dve.wait_ge(S["ph_done"], 12 * b + g + 1)
                    low(pT_l[:, g % 4, 0:w], ps_p[c][:, 0:w], pT_h[:, g % 4, 0:w], S["pl_done"])

            def rows(b, i):
                dve.wait_ge(S["exp_done"], CREDIT + BT * b + i + 1)
                chain.step(dve.reciprocal(row_inv[:, i:i + 1], row_sum[:, i:i + 1]))
                chain.wait()
                dve.wait_ge(S["pv_done"], CREDIT + BT * b + i + 1)
                dve.wait_ge(S["vf_done"], CREDIT + 2 * b + i // MT + 1)
                if i % MT == 0:
                    wait_for(dve, S["yn_done"], CREDIT + 2 * b + i // MT - 1)
                chain.step(dve.scalar_tensor_tensor(
                    out=y[:, i, :], in0=ps_y[:, D:2 * D], scalar=row_inv[:, i:i + 1],
                    in1=part(v_f, slot(b, N) + i * D, D), op0=ALU.mult, op1=ALU.add))
                chain.wait()
                dve.scalar_tensor_tensor(out=y[:, i, :], in0=ps_y[:, 0:D], scalar=row_inv[:, i:i + 1],
                                         in1=y[:, i, :], op0=ALU.mult, op1=ALU.add).then_inc(S["yrow_done"], 1)
                dve.wait_ge(S["yrow_done"], CREDIT + BT * b + i + 1)
                chain.step(dve.bn_stats(y_stats[:, i % MT, :], y[:, i, :]))
                if i % MT == MT - 1:
                    chain.wait()
                    dve.wait_ge(S["y_rs"], CREDIT + 2 * b + i // MT)
                    dve.tensor_copy(wait_carrier[:, :], y_stats[:, 0, 0:1])
                    for t in range(MT):
                        last = dve.bn_aggr(y_mean_var[:, t, :], y_stats[:, t, :])
                    last.then_inc(S["y_stat"], 1)

            def finish_x(b, j):
                dve.wait_ge(S["fc_done"], CREDIT + 2 * b + j + 1)
                dve.wait_ge(S["xb_done"], 2 * b + j + 1)
                dve.tensor_tensor(x[:, bass.ds(b * BT + j * MT, MT), :],
                                  ps_t[:, :].rearrange("p (t d) -> p t d", t=MT), x_bfc[:, :, :], ALU.add)\
                    .then_inc(S["xa_done"], 1)

            def step_a(n, b, more):
                def side_at(place):
                    unit = side_unit(n, b, more, place)
                    if unit:
                        side(*unit)
                side_at(0)
                pT_low(*at(n, b))
                side_at(1)
                if n + 2 < BT or more:
                    maximum(*at(n + 2, b))
                if n == 4 and not more:
                    for t in range(MT + 1):
                        statistics(MACROS, 0, t)
                if n == 4:
                    side_at(2)
                if (n != BT or begun(b)):
                    rows(*at(n - 1, b))
                if n == 7 and not more:
                    for half in range(2):
                        x_low(MACROS, 0, half)
                if n != 4:
                    side_at(2)

            dve.memset(xn[:, :, D - 1:D], 1.0).then_inc(S["setup_dve"], 1)
            dve.wait_ge(S["x_first"], 16)
            for t in range(MT + 1):
                statistics(0, 0, t)
            dve.wait_ge(S["small_in"], 32)
            dve.tensor_scalar(wg_rows[:, 0:D - 1], wg_rows[:, 0:D - 1], wg_rows[:, D - 1:D], None, ALU.subtract)\
                .then_inc(S["wprep"], 1)
            def w1_chunk(c):
                cs = slice(c * 2 * MT, (c + 1) * 2 * MT)
                dve.wait_ge(S[f"w1_in{c}"], 16)
                dve.tensor_copy(last_col[:, cs], w1_rows[:, cs, D - 1]).then_inc(S["last_col"], 1)
                dve.wait_ge(S["last_col"], c + 1)
                if c % 2:
                    dve.tensor_tensor(w1_rows[:, cs, 0:D - 1], w1_rows[:, cs, 0:D - 1],
                                      last_col[:, cs, None].to_broadcast([P, 2 * MT, D - 1]),
                                      ALU.subtract).then_inc(S["w1_sub_dve"], 1)
                if c == 0:
                    dve.wait_ge(S["wprep"], 1)
                    dve.memset(wg_rows[:, D - 1:D], 0.0).then_inc(S["wprep"], 1)
                    dve.wait_ge(S["b1_t"], 1)
                dve.tensor_copy(w1_rows[:, cs, D - 1], ps_g[:, cs]).then_inc(S["b1_put"], 1)

            for c in range(3):
                w1_chunk(c)
            for half in range(2):
                x_low(0, 0, half)
            for e in range(E):
                dve.wait_ge(S["w_hi"], e + 1)
                low(w1_l[:, e, :], ps_h[:, e % RING, :], w1_h[:, e, :], S["w_lo"])
                if e == 0:
                    dve.wait_ge(S["wg_hi"], 1)
                    low(wg_l, ps_lg[:, 0:E], wg_h, S["wg_lo"])
                    w1_chunk(3)
                if e == 2:
                    dve.wait_ge(S["const_ones"], 3 + E)
                for part_no in ((), (), (), (1,), (2, 3), (4,), (5, 6), (7, 8))[e]:
                    route(part_no, 0, 0)
            dve.wait_ge(S["wo_hi"], 1)
            low(wo_l, ps_y[:, 0:HC * D].rearrange("p (c d) -> p c d", c=HC), wo_h, S["wo_lo"])
            dve.wait_ge(S["rows_in"], 64)
            dve.tensor_tensor(bfc_rows[:, :], ps_y[:, HC * D:(HC + 1) * D], bfc_rows[:, :], ALU.add)\
                .then_inc(S["fc_prep"], 1)
            for part_no in range(9, 12):
                route(part_no, 0, 0)
            dve.wait_ge(S["x_rest"], 16)
            ffn_steps(0, make_step(0), chain, dve.Fori)
            first(("xT", 1))
            first(("v", 0))
            finish_low(6, TILES - 2)
            finish(6, TILES - 2)
            first(("q", 1))
            first(("k", 1))
            g_low(TILES - 1)
            first(("v", 1))

            maximum(0, 0)
            finish_low(7, TILES - 1)
            finish(7, TILES - 1)
            maximum(0, 1)
            finished_statistics(TILES - 2)
            finished_statistics(TILES - 1)
            mean_variance(3 * BT, TILES)
            attention_steps(step_a, chain, dve.Fori)
            rows(B - 1, BT - 1)
            for part_no in range(1, 12):
                route(part_no, MACROS, 0)
            side(("fc", 0), B - 1)

            ffn_steps(1, make_step(1), chain, dve.Fori)
            finish_low(6, 2 * TILES - 2)
            finish(6, TILES - 2)
            g_low(2 * TILES - 1)
            finish_low(7, 2 * TILES - 1)
            finish(7, TILES - 1)


_INS = ["L0_attn_x", "L0_attn_Wq", "L0_attn_Wk", "L0_attn_Wv", "L0_attn_Wfc", "L0_attn_bfc", "L0_attn_gamma",
        "L0_attn_beta", "L0_ffn_Wg", "L0_ffn_W1", "L0_ffn_b1", "L0_ffn_Wo", "L0_ffn_bo"]


def kernel(**inputs):
    import numpy as _np
    import concourse.bacc as _bacc
    from concourse import mybir as _mybir
    from concourse.bass_utils import run_bass_kernel_spmd as _run

    nc = _bacc.Bacc("TRN2", target_bir_lowering=False, num_devices=1)
    arrays, args = {}, []
    for name in _INS:
        a = _np.ascontiguousarray(inputs[name])
        arrays[f"in_{name}_dram"] = a
        args.append(nc.dram_tensor(f"in_{name}_dram", a.shape, _mybir.dt.from_np(a.dtype), kind="ExternalInput").ap())
    shape = inputs["L0_attn_x"].shape
    args.append(nc.dram_tensor("out_0_dram", shape, _mybir.dt.float32, kind="ExternalOutput").ap())
    macaron_kernel(nc, *args)
    r = _run(nc, [arrays], core_ids=[0])
    return r.results[0]["out_0_dram"]
```
